# Optimizing a Trainium2 kernel written in Bass

```python
import numpy as np
import jax
import jax.numpy as jnp

def _softmax(x, axis=-1):
    return jax.nn.softmax(x, axis=axis)

def _gelu(x):
    return jax.nn.gelu(x, approximate=True)

def _silu(x):
    return jax.nn.silu(x)

def _sigmoid(x):
    return jax.nn.sigmoid(x)

def _layernorm(x, axis=-1, eps=1e-05):
    m = jnp.mean(x, axis=axis, keepdims=True)
    v = jnp.var(x, axis=axis, keepdims=True)
    return (x - m) / jnp.sqrt(v + eps)

def _scatter_add(tgt, idx, src, axis=0):
    return tgt.at[idx].add(src)

def _segment_sum(src, seg, n):
    return jax.ops.segment_sum(src, seg, n)
kernel_name = 'mk_flamingo_gated_d1_seqx_r4_cdcfcd'

def setup_inputs(seed: int=0):
    np.random.seed(seed)
    _w = jnp.asarray

    def _rec_inputs():
        import jax
        import jax.numpy as jnp
        _rk = jax.random.key(seed)
        x = 7.22e-05 + 1 * jax.random.normal(jax.random.fold_in(_rk, 1), (4, 512, 512), jnp.float32)
        _lenS = 512 - jax.random.randint(jax.random.fold_in(_rk, 7), (4,), 0, max(1, 512 // 4) + 1, jnp.int32)
        _lenS2 = 512 - jax.random.randint(jax.random.fold_in(_rk, 8), (4,), 0, max(1, 512 // 4) + 1, jnp.int32)
        _ctx_1024P = jax.random.normal(jax.random.fold_in(_rk, 11), (4, 16, 256), jnp.float32)
        _ctx_1024c = jax.random.dirichlet(jax.random.fold_in(_rk, 511), 0.3 * jnp.ones((16,), jnp.float32), (4, 512))
        _ctx_1024t = jnp.einsum('bsk,bkd->bsd', _ctx_1024c, _ctx_1024P)
        _ctx_1024t = _ctx_1024t * jax.lax.rsqrt(jnp.mean(jnp.square(_ctx_1024t)) + 1e-12) * 0.953939
        ctx_1024 = 2.81802e-05 + 1.00001 * (_ctx_1024t + 0.3 * jax.random.normal(jax.random.fold_in(_rk, 611), (4, 512, 256), jnp.float32))
        _g = jax.random.normal(jax.random.fold_in(_rk, 9001), (2, 1), jnp.float32)
        _g = jnp.sign(_g) * jnp.maximum(jnp.abs(_g), 1.0) + (_g == 0) * 1.0
        g_xattn = _g[0]
        g_ffn = _g[1]
        return (x, ctx_1024, g_xattn, g_ffn)
    x, ctx_1024, g_xattn, g_ffn = _rec_inputs()

    def _L0_xattn_setup():
        import jax, jax.numpy as jnp
        import numpy as np
        key = jax.random.key(seed)
        ks = jax.random.split(key, 6)
        B, L, N, C, D = (8, 128, 512, 256, 128)
        return {'teacher_logits': jax.random.normal(ks[0], (B, L, N), dtype=jnp.float32), 'teacher_features': jax.random.normal(ks[1], (B, N, C), dtype=jnp.float32), 'Wq': jax.random.normal(ks[2], (D, C), dtype=jnp.float32) * (1.0 / np.sqrt(C)), 'bq': jnp.zeros((D,), dtype=jnp.float32), 'Wk': jax.random.normal(ks[3], (D, C), dtype=jnp.float32) * (1.0 / np.sqrt(C)), 'bk': jnp.zeros((D,), dtype=jnp.float32)}
    _L0_xattn_all = _L0_xattn_setup()
    _L0_xattn_in = {k: v for k, v in _L0_xattn_all.items() if k in ('Wq', 'bq', 'Wk', 'bk')}
    del _L0_xattn_all

    def _L0_ffn_setup():
        import jax, jax.numpy as jnp
        import numpy as np
        D = 512
        H = 352
        E = 8
        TOP_K = 2
        B, S = (4, 512)

        def _swiglu(x, Wg, Wu, Wd):
            return jax.nn.silu(x @ Wg) * (x @ Wu) @ Wd
        key = jax.random.key(seed)
        ks = jax.random.split(key, 10)
        sc = 0.02
        x = jax.random.normal(ks[0], (B, S, D), dtype=jnp.float32)
        Wg_s = jax.random.normal(ks[1], (D, H), dtype=jnp.float32) * sc
        Wu_s = jax.random.normal(ks[2], (D, H), dtype=jnp.float32) * sc
        Wd_s = jax.random.normal(ks[3], (H, D), dtype=jnp.float32) * sc
        Wg = jax.random.normal(ks[4], (E, D, H), dtype=jnp.float32) * sc
        Wu = jax.random.normal(ks[5], (E, D, H), dtype=jnp.float32) * sc
        Wd = jax.random.normal(ks[6], (E, H, D), dtype=jnp.float32) * sc
        Wr = jax.random.normal(ks[7], (D, E), dtype=jnp.float32) * sc
        br = jax.random.normal(ks[8], (E,), dtype=jnp.float32) * sc
        rb = jnp.zeros((E,), dtype=jnp.float32)
        return {'x': x, 'Wg_s': Wg_s, 'Wu_s': Wu_s, 'Wd_s': Wd_s, 'Wg': Wg, 'Wu': Wu, 'Wd': Wd, 'Wr': Wr, 'br': br, 'rb': rb}
    _L0_ffn_all = _L0_ffn_setup()
    _L0_ffn_in = {k: v for k, v in _L0_ffn_all.items() if k in ('Wg_s', 'Wu_s', 'Wd_s', 'Wg', 'Wu', 'Wd', 'Wr', 'br', 'rb')}
    del _L0_ffn_all
    return {'x': x, 'ctx_1024': ctx_1024, 'g_xattn': g_xattn, 'g_ffn': g_ffn, 'L0_xattn_Wq': _L0_xattn_in['Wq'], 'L0_xattn_bq': _L0_xattn_in['bq'], 'L0_xattn_Wk': _L0_xattn_in['Wk'], 'L0_xattn_bk': _L0_xattn_in['bk'], 'L0_ffn_Wg_s': _L0_ffn_in['Wg_s'], 'L0_ffn_Wu_s': _L0_ffn_in['Wu_s'], 'L0_ffn_Wd_s': _L0_ffn_in['Wd_s'], 'L0_ffn_Wg': _L0_ffn_in['Wg'], 'L0_ffn_Wu': _L0_ffn_in['Wu'], 'L0_ffn_Wd': _L0_ffn_in['Wd'], 'L0_ffn_Wr': _L0_ffn_in['Wr'], 'L0_ffn_br': _L0_ffn_in['br'], 'L0_ffn_rb': _L0_ffn_in['rb']}

def reference(x, ctx_1024, g_xattn, g_ffn, L0_xattn_Wq, L0_xattn_bq, L0_xattn_Wk, L0_xattn_bk, L0_ffn_Wg_s, L0_ffn_Wu_s, L0_ffn_Wd_s, L0_ffn_Wg, L0_ffn_Wu, L0_ffn_Wd, L0_ffn_Wr, L0_ffn_br, L0_ffn_rb):
    import jax
    import jax.numpy as jnp

    def _L0_xattn_ref(teacher_logits, teacher_features, Wq, bq, Wk, bk):
        import jax, jax.numpy as jnp
        import numpy as np
        query = jnp.einsum('bnc,dc->bnd', teacher_features, Wq) + bq
        key = jnp.einsum('bnc,dc->bnd', teacher_features, Wk) + bk
        energy = jnp.einsum('bnd,bmd->bnm', query, key)
        attention = jax.nn.softmax(energy, axis=-1)
        x_m = jnp.einsum('bln,bmn->blm', teacher_logits, attention)
        return x_m

    def _L0_ffn_ref(x, Wg_s, Wu_s, Wd_s, Wg, Wu, Wd, Wr, br, rb):
        import jax, jax.numpy as jnp
        import numpy as np
        D = 512
        H = 352
        E = 8
        TOP_K = 2
        B, S = (4, 512)

        def _swiglu(x, Wg, Wu, Wd):
            return jax.nn.silu(x @ Wg) * (x @ Wu) @ Wd
        shared_out = _swiglu(x, Wg_s, Wu_s, Wd_s)
        logits = x @ Wr + br + rb
        probs = jax.nn.sigmoid(logits)
        top_v, top_i = jax.lax.top_k(probs, TOP_K)
        top_v = top_v / jnp.sum(top_v, axis=-1, keepdims=True)
        w = jnp.sum(top_v[..., None] * jax.nn.one_hot(top_i, E, dtype=x.dtype), axis=-2)
        routed_out = jnp.zeros_like(x)
        for e in range(E):
            routed_out = routed_out + _swiglu(x, Wg[e], Wu[e], Wd[e]) * w[..., e:e + 1]
        return shared_out + routed_out
    x = x + jnp.tanh(g_xattn[0]) * _L0_xattn_ref(_layernorm(x, axis=-1), ctx_1024, L0_xattn_Wq, L0_xattn_bq, L0_xattn_Wk, L0_xattn_bk)
    x = x + jnp.tanh(g_ffn[0]) * _L0_ffn_ref(_layernorm(x, axis=-1), L0_ffn_Wg_s, L0_ffn_Wu_s, L0_ffn_Wd_s, L0_ffn_Wg, L0_ffn_Wu, L0_ffn_Wd, L0_ffn_Wr, L0_ffn_br, L0_ffn_rb)
    return x

_drawn_inputs = setup_inputs


def setup_inputs(seed=0):
    import zlib

    import numpy as np

    out = dict(_drawn_inputs(seed))
    spreads = {'L0_xattn_bq': (0.0, 0.1), 'L0_xattn_bk': (0.0, 0.1), 'L0_ffn_rb': (0.0, 0.1)}
    factors = {}
    for name, (base, spread) in spreads.items():
        noise = np.random.default_rng([zlib.crc32(name.encode()), seed]).standard_normal(out[name].shape)
        drawn = base * np.exp(spread * noise) if base else spread * noise
        out[name] = jnp.asarray(drawn.astype(out[name].dtype))
    for name, factor in factors.items():
        out[name] = (out[name] * factor).astype(out[name].dtype)
    return out
```

```python
from contextlib import ExitStack

import concourse.bass as bass
from concourse import mybir

F32 = mybir.dt.float32
F16 = mybir.dt.float16
U32 = mybir.dt.uint32
I32 = mybir.dt.int32
ALU = mybir.AluOpType
ACT = mybir.ActivationFunctionType
AX_X = mybir.AxisListType.X

P = 128
EPS = 1e-5
WSCALE = 64.0
YSCALE = 1.0 / (WSCALE * WSCALE)
HI, LO = 0, 1


def flamingo_block(nc, x, ctx_in, g_x, g_f, wq, bq, wk, bk, wg_s, wu_s, wd_s, wg, wu, wd, wr, br, rb, out):
    B, S, D = x.shape
    C = ctx_in.shape[2]
    E, _, H = wg.shape
    T = B * S
    NQ = S // P
    NT = T // P
    DC = D // P
    CC = C // P
    HC = -(-H // P)
    HK = [min(P, H - P * j) for j in range(HC)]
    TOPK = 2
    NR = (TOPK * T + E * (P - 1)) // P
    NB = NT + NR
    assert (S, D, C, wq.shape[0], DC, NQ) == (512, 512, 256, P, 4, 4) and NT % 2 == 0 and NR % 2 == 1

    GU_N = 2 * (DC // 2) * H
    DN_N = HC * (D // 2)
    HALF = GU_N + DN_N
    SLOT = 4 * HALF
    SHARED = E

    out_t = out[0:T, :].rearrange("(n p) d -> n p d", p=P)
    x_v = x.rearrange("b (q p) d -> b p q d", p=P)
    ctx_v = ctx_in.rearrange("b (q p) c -> b p q c", p=P)
    x2n_rows = nc.dram_tensor("x2n_rows", [T, D], F32).ap()
    x2n_t = x2n_rows.rearrange("(n p) d -> n p d", p=P)

    es = ExitStack()
    with es:
        def sb(name, shape, dt=F32):
            return es.enter_context(nc.sbuf_tensor(name, shape, dt))

        def sem(name):
            return es.enter_context(nc.semaphore(name))

        banks = [es.enter_context(nc.psum_tensor(f"bank{i}", [P, 512], F32)) for i in range(8)]
        EB, TP, XM, LG, RB = banks[0:2], banks[2:4], banks[4:6], banks[6], banks[7]
        PG, PU, PXT, PHT, PY = XM[0], XM[1], TP[0], TP[1], EB[0]

        W = sb("W", [P, (E + 1) * SLOT], F16)
        over32 = W[:, 0:E * SLOT].bitcast(F32)
        at = [0]

        def carve(n):
            at[0] += n
            return at[0] - n

        def o32(n):
            o = carve(n)
            return over32[:, o:o + n]

        AT0 = 2 * carve(B * DC * S)
        XNT0 = 2 * carve(B * DC * S)
        ABS = 2 * DC * S
        ctx_sb = o32(NQ * C).rearrange("p (q c) -> p q c", q=NQ)
        ctxT = o32(CC * S).rearrange("p (c n) -> p c n", c=CC)
        qT, kT = o32(S), o32(S)
        prob = o32(2 * S).rearrange("p (i n) -> p i n", i=2)
        xn = o32(2 * D).rearrange("p (i n) -> p i n", i=2)
        x2 = o32(2 * D).rearrange("p (i n) -> p i n", i=2)
        x2n = o32(2 * D).rearrange("p (i n) -> p i n", i=2)
        xT2_0 = 2 * carve(2 * D)
        xT2 = W[:, xT2_0:xT2_0 + 4 * D].rearrange("p (i l n) -> p i l n", i=2, l=2)
        X0 = E * SLOT // 2 - B * NQ * D
        assert at[0] <= X0
        x_sb = over32[:, X0:X0 + B * NQ * D]

        rt = [at[0]]

        def r32(n):
            rt[0] += n
            assert rt[0] <= E * SLOT // 2
            return over32[:, rt[0] - n:rt[0]]

        def r16(n):
            return r32((n + 1) // 2).bitcast(F16)

        TE = NT * E
        KT_N = TOPK * NT
        logits = sb("logits", [P, TE])
        lrb, pr = r32(TE), r32(TE)
        beats, ties = r32(TE * E), r32(TE * E)
        rank = r32(TE)
        selk, prodk = r32(TOPK * TE), r32(TOPK * TE)
        topv, wk_f = r32(KT_N), r32(KT_N)
        vsum, vinv = r32(NT), r32(NT)
        sel16 = r16(TE)
        whi, wlo = r16(KT_N), r16(KT_N)
        cgt, endm = r32(E * NT), r32(E * E)
        nblk, endb, startb = r32(E), r32(E), r32(E)
        slot_te, slotk = r32(TE), r32(KT_N)
        slot_i, lane_i, blk_i = (r32(KT_N).bitcast(I32) for _ in range(3))
        lane1h = r16(KT_N * P).rearrange("p (i l) -> p i l", l=P)
        blk1h = r16(KT_N * 4 * NR).rearrange("p (i f n) -> p i f n", f=4, n=NR)
        tgt_f, w_f = r32(NR), r32(NR)
        eb_m, eb_f = r32(NR * E), r32(NR)

        tok = sb("tok", [P, NB], U32)
        tgt = sb("tgt", [P, NB], U32)
        wcol = sb("wcol", [P, NB])
        eoff = sb("eoff", [1, NB], I32)

        stage = sb("stage", [P, 2, HALF])
        xg = sb("xg", [P, 2, D])
        xT = sb("xT", [P, 2, D], F16)
        silu_g = sb("silu_g", [P, H])
        h = sb("h", [P, HC * P])
        hT = sb("hT", [P, 2, HC * P], F16)
        y = sb("y", [P, 2, D])
        idx_g = sb("idx_g", [P, 2], U32)
        idx_s = sb("idx_s", [P, 2], U32)

        ident = sb("ident", [P, P])
        ones16 = sb("ones16", [P, P], F16)
        tri16 = sb("tri16", [P, P], F16)
        lane_iota = sb("lane_iota", [P, P])
        cnt_iota = sb("cnt_iota", [P, NT])
        tri_lt = sb("tri_lt", [P, E, E])
        tri_le = sb("tri_le", [P, E, E])
        tok_id = sb("tok_id", [P, KT_N])
        pad_row = sb("pad_row", [P, 1])
        pad_neg = sb("pad_neg", [P, 1])
        mhalf = sb("mhalf", [P, NQ])
        wqk = sb("wqk", [P, 2, C])
        wqkT = sb("wqkT", [P, 2, CC, P])
        bqk = sb("bqk", [P, 2])
        gates = sb("gates", [P, 2])
        tanh_g = sb("tanh_g", [P, 2])
        gff = sb("gff", [P, 1])
        br_sb, rb_sb = sb("br_sb", [P, E]), sb("rb_sb", [P, E])
        wr_sb = sb("wr_sb", [P, DC, E])
        wr16 = sb("wr16", [P, 2, DC, E], F16)

        st1, mv1 = sb("st1", [P, NQ, 6]), sb("mv1", [P, NQ, 2])
        ve1, nm1, rstd1, nb1 = (sb(n, [P, NQ]) for n in ("ve1", "nm1", "rstd1", "nb1"))
        st2, mv2 = sb("st2", [P, 2, 6]), sb("mv2", [P, 2, 2])
        ve2, nm2, rstd2, nb2 = (sb(n, [P, 2]) for n in ("ve2", "nm2", "rstd2", "nb2"))
        negmax, rowsum, rinv = (sb(n, [P, NQ]) for n in ("negmax", "rowsum", "rinv"))

        s_const = sem("s_const")
        s_par = sem("s_par")
        s_x = sem("s_x")
        s_ctx = sem("s_ctx")
        s_wT, s_wTc = sem("s_wT"), sem("s_wTc")
        s_tanh, s_gff = sem("s_tanh"), sem("s_gff")
        s_wrh, s_wrl = sem("s_wrh"), sem("s_wrl")
        s_eb, s_ef = sem("s_eb"), sem("s_ef")
        s_xnt, s_pt, s_xt2 = sem("s_xnt"), sem("s_pt"), sem("s_xt2")
        s_hi, s_lo = sem("s_hi"), sem("s_lo")
        s_max, s_rec, s_pn = sem("s_max"), sem("s_rec"), sem("s_pn")
        s_bn1, s_ag1, s_v1 = sem("s_bn1"), sem("s_ag1"), sem("s_v1")
        s_bn2, s_ag2, s_v2 = sem("s_bn2"), sem("s_ag2"), sem("s_v2")
        s_pow1, s_n1 = sem("s_pow1"), sem("s_n1")
        s_pow2, s_n2 = sem("s_pow2"), sem("s_n2")
        s_xn, s_x2n = sem("s_xn"), sem("s_x2n")
        s_xm, s_x2 = sem("s_xm"), sem("s_x2")
        s_lg, s_lgf = sem("s_lg"), sem("s_lgf")
        s_st_x2 = [sem("s_st_x2_0"), sem("s_st_x2_1")]
        s_st_n = [sem("s_st_n_0"), sem("s_st_n_1")]
        s_pad = sem("s_pad")
        s_ch = sem("s_ch")
        s_lrb, s_ex = sem("s_lrb"), sem("s_ex")
        s_sel, s_pos, s_1h, s_tab = sem("s_sel"), sem("s_pos"), sem("s_1h"), sem("s_tab")
        s_route = sem("s_route")
        s_stg = [sem("s_stg_0"), sem("s_stg_1")]
        s_cvh, s_cvl = sem("s_cvh"), sem("s_cvl")
        s_zero = sem("s_zero")
        s_idxg, s_idxs = sem("s_idxg"), sem("s_idxs")
        s_xg = [sem("s_xg_0"), sem("s_xg_1")]
        s_xt, s_xth, s_xtl = sem("s_xt"), sem("s_xth"), sem("s_xtl")
        s_gu, s_silu, s_h = sem("s_gu"), sem("s_silu"), sem("s_h")
        s_ht, s_hth, s_htl = sem("s_ht"), sem("s_hth"), sem("s_htl")
        s_apart = sem("s_apart")
        s_dn, s_y = sem("s_dn"), sem("s_y")
        s_sc = sem("s_sc")

        block = es.enter_context(nc.Block())

        def need(eng, s, v):
            if not isinstance(v, int) or v > 0:
                eng.wait_ge(s, v)

        CONSTS = 16

        def wait_apart(eng, s, v):
            eng.wait_ge(s, v)
            eng.sem_inc(s_apart, 1)

        def groups(s2, s1, base):
            per = (2 if s1 is not None else 0) + (1 if s2 is not None else 0)

            def number(kind, q):
                return base + per * q + {"xn": 0, "p": 1, "x2": per - 1}[kind]
            return number

        G1, G2, G3 = 2 * NQ, 3 * NQ, NQ

        def steps(eng, step):
            step(None, 0, 0)
            step(0, 1, G1)
            with eng.Fori(1, B - 1) as b:
                step(b, b + 1, G2 * b + G1)
            step(B - 1, None, G1 + G2 * (B - 1))

        GROUPS = G1 + G2 * (B - 1) + G3

        def par(kind, q, s2, s1):
            return groups(s2, s1, 0)(kind, q) % 2

        def rows(b, q):
            return bass.ds(b * (NQ * D) + q * D, D)

        def xnt(b, hl, q, c=None):
            o = XNT0 + b * ABS + (hl * DC * S + q * D)
            return W[:, bass.ds(o, D)] if c is None else W[:, bass.ds(o + c * P, P)]

        def att(b, hl, c):
            return W[:, bass.ds(AT0 + b * ABS + (hl * DC * S + c * S), S)]

        def att_cols(b, hl, q):
            whole = W[:, bass.ds(AT0 + b * ABS + hl * DC * S, DC * S)]
            return whole.rearrange("p (c m) -> p c m", c=DC)[:, :, q * P:(q + 1) * P]

        def gu_w(off, hl, m, c):
            k, c2 = divmod(c, DC // 2)
            return W[:, bass.ds(off + (k * 2 * HALF + hl * HALF + (m * (DC // 2) + c2) * H), H)]

        def dn_w(off, hl, j):
            whole = W[:, bass.ds(off, SLOT)].rearrange("p (k r) -> p k r", k=2)
            o = hl * HALF + GU_N + j * (D // 2)
            return whole[0:HK[j], :, o:o + D // 2]

        wg_rows, wu_rows, wd_rows = (w.rearrange("e d n -> (e d) n") for w in (wg, wu, wd))

        @block.sync
        def _(sp):
            def stage_half(k, gate, up, down):
                half = stage[:, k, 0:GU_N].rearrange("p (m c n) -> p m c n", m=2, c=DC // 2)
                rest = stage[:, k, GU_N:HALF].rearrange("p (j n) -> p j n", j=HC)
                sp.dma_start(half[:, 0], gate.rearrange("(c p) n -> p c n", p=P)).then_inc(s_stg[k], 16)
                sp.dma_start(half[:, 1], up.rearrange("(c p) n -> p c n", p=P)).then_inc(s_stg[k], 16)
                sp.dma_start(rest[:, 0:HC - 1], down[0].rearrange("(j p) n -> p j n", p=P)).then_inc(s_stg[k], 16)
                sp.dma_start(rest[0:HK[-1], HC - 1], down[1]).then_inc(s_stg[k], 16)

            def load_ctx(b):
                need(sp, s_eb, 8 * (b - 1) + CC)
                sp.dma_start(ctx_sb, ctx_v[b]).then_inc(s_ctx, 16)

            def load_x(b):
                need(sp, s_x, 16 * b)
                sp.dma_start(x_sb[:, b * NQ * D:(b + 1) * NQ * D].rearrange("p (q d) -> p q d", q=NQ),
                             x_v[b]).then_inc(s_x, 16)

            def store(b):
                for q in range(NQ):
                    i = q % 2
                    tile = bass.ds(b * S + q * P, P)
                    sp.wait_ge(s_x2, NQ * b + q + 1)
                    sp.dma_start(out[tile, :], x2[:, i, :]).then_inc(s_st_x2[i], 16)
                    sp.wait_ge(s_x2n, NQ * b + q + 1)
                    sp.dma_start(x2n_rows[tile, :], x2n[:, i, :]).then_inc(s_st_n[i], 16)

            load_ctx(0)
            load_x(0)
            sp.wait_ge(s_zero, 3)
            for k in range(2):
                rows_k = slice(k * (D // 2), (k + 1) * (D // 2))
                stage_half(k, wg_s[rows_k, :], wu_s[rows_k, :],
                           (wd_s[0:(HC - 1) * P, rows_k], wd_s[(HC - 1) * P:H, rows_k]))
            load_x(1)
            load_ctx(1)
            load_x(2)
            load_x(3)
            sp.dma_start(out[T:T + P, :], y[:, 0, :]).then_inc(s_pad, 16)
            for b in range(2):
                load_ctx(b + 2)
                store(b)
            with sp.Fori(2, B) as b:
                store(b)
            with sp.Fori(0, E) as e:
                for k in range(2):
                    sp.wait_ge(s_cvl, 2 * e + k + 1)
                    cols = slice(k * (D // 2), (k + 1) * (D // 2))
                    rows_k = bass.ds(e * D + k * (D // 2), D // 2)
                    stage_half(k, wg_rows[rows_k, :], wu_rows[rows_k, :],
                               (wd_rows[bass.ds(e * H, (HC - 1) * P), cols],
                                wd_rows[bass.ds(e * H + (HC - 1) * P, HK[-1]), cols]))
            sp.wait_ge(s_pad, 16)
            sp.wait_ge(s_sc, 16 * NB)

        @block.gpsimd
        def _(pool):
            g = nc.gpsimd
            iota = dict(allow_small_or_imprecise_dtypes=True)
            g.memset(ident[:, :], 0.0).then_inc(s_const, 1)
            g.memset(ones16[:, :], 1.0).then_inc(s_const, 1)
            g.memset(mhalf[:, :], -0.5).then_inc(s_const, 1)
            g.memset(tri_lt[:, :, :], 1.0).then_inc(s_const, 1)
            g.memset(tri_le[:, :, :], 1.0).then_inc(s_const, 1)
            g.iota(lane_iota[:, :], [[1, P]], base=0, channel_multiplier=0, **iota).then_inc(s_const, 1)
            g.iota(cnt_iota[:, :], [[P, NT]], base=0, channel_multiplier=0, **iota).then_inc(s_const, 1)
            g.iota(tok_id[:, :], [[0, TOPK], [P, NT]], base=0, channel_multiplier=1, **iota).then_inc(s_const, 1)
            g.iota(pad_row[:, :], [[0, 1]], base=T, channel_multiplier=1, **iota).then_inc(s_const, 1)
            g.iota(pad_neg[:, :], [[0, 1]], base=-T, channel_multiplier=-1, **iota).then_inc(s_const, 1)
            g.iota(tok[:, 0:NT], [[P, NT]], base=0, channel_multiplier=1).then_inc(s_const, 1)
            g.iota(tgt[:, 0:NT], [[P, NT]], base=0, channel_multiplier=1).then_inc(s_const, 1)
            pool.wait_ge(s_const, 12)
            g.affine_select(out=ident[:, :], in_=ident[:, :], compare_op=ALU.not_equal, fill=1.0,
                            base=0, pattern=[[-1, P]], channel_multiplier=1).then_inc(s_const, 1)
            g.affine_select(out=tri16[:, :], in_=ones16[:, :], compare_op=ALU.is_gt, fill=0.0,
                            base=0, pattern=[[1, P]], channel_multiplier=-1).then_inc(s_const, 1)
            g.affine_select(out=tri_lt[:, :, :], in_=tri_lt[:, :, :], compare_op=ALU.is_gt, fill=0.0,
                            base=0, pattern=[[1, E], [-1, E]], channel_multiplier=0).then_inc(s_const, 1)
            g.affine_select(out=tri_le[:, :, :], in_=tri_le[:, :, :], compare_op=ALU.is_ge, fill=0.0,
                            base=0, pattern=[[1, E], [-1, E]], channel_multiplier=0).then_inc(s_const, 1)
            pool.wait_ge(s_const, CONSTS)

            def step(s2, s1, base):
                if s1 is not None:
                    pool.wait_ge(s_v1, s1 + 1)
                    need(pool, s_xn, NQ * s1)
                    g.tensor_tensor(rstd1[:, :], ve1[:, :], mhalf[:, :], ALU.pow).then_inc(s_pow1, 1)
                    pool.wait_ge(s_pow1, s1 + 1)
                    g.tensor_tensor(nb1[:, :], nm1[:, :], rstd1[:, :], ALU.mult).then_inc(s_n1, 1)
                if s2 is not None:
                    for q in range(NQ):
                        i = slice(q % 2, q % 2 + 1)
                        pool.wait_ge(s_v2, NQ * s2 + q + 1)
                        need(pool, s_x2n, NQ * s2 + q - 1)
                        g.tensor_tensor(rstd2[:, i], ve2[:, i], mhalf[:, 0:1], ALU.pow).then_inc(s_pow2, 1)
                        pool.wait_ge(s_pow2, NQ * s2 + q + 1)
                        g.tensor_tensor(nb2[:, i], nm2[:, i], rstd2[:, i], ALU.mult).then_inc(s_n2, 1)

            steps(pool, step)

            def gather(n, i):
                need(pool, s_xt, n - 1)
                g.tensor_copy(idx_g[:, i:i + 1], tok[:, bass.ds(n, 1)]).then_inc(s_idxg, 1)
                wait_apart(pool, s_idxg, n + 1)
                g.indirect_dma_start(xg[:, i, :], None, x2n_rows,
                                     bass.IndirectOffsetOnAxis(ap=idx_g[:, i:i + 1], axis=0)).then_inc(s_xg[i], 16)

            def scatter(n, i):
                g.tensor_copy(idx_s[:, i:i + 1], tgt[:, bass.ds(n, 1)]).then_inc(s_idxs, 1)
                pool.wait_ge(s_idxs, n + 1)
                need(pool, s_sc, 16 * n)
                wait_apart(pool, s_y, n + 1)
                g.indirect_dma_start(out, bass.IndirectOffsetOnAxis(ap=idx_s[:, i:i + 1], axis=0), y[:, i, :],
                                     None, compute_op=ALU.add).then_inc(s_sc, 16)

            for i in range(2):
                pool.wait_ge(s_st_n[i], 16 * NT // 2)
                pool.wait_ge(s_st_x2[i], 16 * NT // 2)
            pool.wait_ge(s_pad, 16)
            pool.wait_ge(s_route, 1)
            LEAD = 4
            for n in range(LEAD):
                gather(n, n % 2)
            for n in range(2):
                scatter(n, n % 2)
                gather(n + LEAD, n % 2)
            with pool.Fori(2, NB - LEAD - 1, 2) as n2:
                for i in range(2):
                    scatter(n2 + i, i)
                    gather(n2 + i + LEAD, i)
            for n in range(NB - LEAD - 1, NB):
                scatter(n, n % 2)
                if n + LEAD < NB:
                    gather(n + LEAD, n % 2)

        @block.scalar
        def _(act):
            a = nc.scalar
            for dst, src in ((wqk[:, 0, :], wq), (wqk[:, 1, :], wk),
                             (bqk[:, 0:1], bq.rearrange("(p a) -> p a", a=1)), (bqk[:, 1:2], bk.rearrange("(p a) -> p a", a=1)),
                             (gates[:, 0:1], g_x.partition_broadcast(P)), (gates[:, 1:2], g_f.partition_broadcast(P)),
                             (br_sb[:, :], br.partition_broadcast(P)), (rb_sb[:, :], rb.partition_broadcast(P)),
                             (wr_sb[:, :, :], wr.rearrange("(c p) e -> p c e", p=P))):
                act.dma_start(dst, src).then_inc(s_par, 16)
            act.wait_ge(s_par, 16 * 9)
            a.activation(tanh_g[:, :], gates[:, :], ACT.Tanh).then_inc(s_tanh, 1)
            a.activation(wr16[:, HI], wr_sb[:, :, :], ACT.Copy, scale=WSCALE).then_inc(s_wrh, 1)
            act.wait_ge(s_wT, 1)
            a.activation(wqkT[:, :, :, :].rearrange("p a c d -> p (a c d)"), RB[:, 0:2 * C], ACT.Copy).then_inc(s_wTc, 1)

            def split_hi(dst, src):
                a.activation(dst, src, ACT.Copy).then_inc(s_hi, 1)

            def step(s2, s1, base):
                if s1 is not None:
                    for c in range(CC):
                        act.wait_ge(s_eb, 8 * s1 + c + 1)
                        a.activation(ctxT[:, c, :], EB[c][:, :], ACT.Copy).then_inc(s_ef, 1)
                    for m, dst in enumerate((qT, kT)):
                        act.wait_ge(s_eb, 8 * s1 + CC + m + 1)
                        a.activation(dst, EB[m][:, :], ACT.Identity, bias=bqk[:, m:m + 1]).then_inc(s_ef, 1)
                for q in range(NQ):
                    i = q % 2
                    if s1 is not None:
                        if q == 0:
                            act.wait_ge(s_n1, s1 + 1)
                        need(act, s_xnt, NQ * s1 + q - 1)
                        a.activation(xn[:, i, :], x_sb[:, rows(s1, q)], ACT.Identity, bias=nb1[:, q:q + 1],
                                     scale=rstd1[:, q:q + 1]).then_inc(s_xn, 1)
                        act.wait_ge(s_max, NQ * s1 + q + 1)
                        need(act, s_pt, NQ * s1 + q - 1)
                        a.activation(prob[:, i, :], EB[i][:, :], ACT.Exp, bias=negmax[:, q:q + 1],
                                     accum_out=rowsum[:, q:q + 1]).then_inc(s_ef, 1)
                        act.wait_ge(s_xnt, NQ * s1 + q + 1)
                        split_hi(xnt(s1, HI, q), TP[par("xn", q, s2, s1)][:, :])
                        act.wait_ge(s_rec, NQ * s1 + q + 1)
                        a.activation(prob[:, i, :], prob[:, i, :], ACT.Copy, scale=rinv[:, q:q + 1]).then_inc(s_pn, 1)
                        act.wait_ge(s_pt, NQ * s1 + q + 1)
                        split_hi(att_cols(s1, HI, q), TP[par("p", q, s2, s1)][:, :].rearrange("p (c m) -> p c m", c=DC))
                    if s2 is not None:
                        act.wait_ge(s_n2, NQ * s2 + q + 1)
                        need(act, s_xt2, NQ * s2 + q - 1)
                        need(act, s_st_n[i], 16 * (NQ // 2 * s2 + q // 2))
                        a.activation(x2n[:, i, :], x2[:, i, :], ACT.Identity, bias=nb2[:, i:i + 1],
                                     scale=rstd2[:, i:i + 1]).then_inc(s_x2n, 1)
                        act.wait_ge(s_xt2, NQ * s2 + q + 1)
                        need(act, s_lg, NQ * s2 + q - 1)
                        split_hi(xT2[:, i, HI, :], TP[par("x2", q, s2, s1)][:, :])

            steps(act, step)

            def convert(slot, k, loads):
                act.wait_ge(s_stg[k], 64 * loads)
                dst = W[:, bass.ds(slot * SLOT + k * 2 * HALF, HALF)]
                a.activation(dst, stage[:, k, :], ACT.Copy, scale=WSCALE).then_inc(s_cvh, 1)

            for k in range(2):
                convert(SHARED, k, 1)
            act.wait_ge(s_lrb, 1)
            a.activation(pr, lrb, ACT.Exp, scale=-1.0).then_inc(s_ex, 1)

            def xT_hi(n):
                act.wait_ge(s_xt, n + 1)
                a.activation(xT[:, HI, :], PXT[:, :], ACT.Copy).then_inc(s_xth, 1)

            def y_out(n, i):
                act.wait_ge(s_dn, n + 1)
                need(act, s_sc, 16 * (n - 1))
                a.activation(y[:, i, :], PY[:, :], ACT.Copy, scale=wcol[:, bass.ds(n, 1)]).then_inc(s_y, 1)

            def blk(n, i, first=False, last=False):
                act.wait_ge(s_gu, n + 1)
                need(act, s_h, n)
                a.activation(silu_g[:, :], PG[:, 0:H], ACT.Silu, scale=1.0 / WSCALE).then_inc(s_silu, 1)
                if not last:
                    xT_hi(n + 1)
                if not first:
                    y_out(n - 1, 1 - i)
                act.wait_ge(s_ht, n + 1)
                a.activation(hT[:, HI, :], PHT[:, 0:HC * P], ACT.Copy).then_inc(s_hth, 1)

            act.wait_ge(s_route, 1)
            act.wait_ge(s_pad, 16)
            xT_hi(0)
            for n in range(4):
                blk(n, n % 2, first=(n == 0))
                convert(n // 2, n % 2, n // 2 + 2)
            with act.Fori(2, E) as e:
                for k in range(2):
                    blk(2 * e + k, k)
                    convert(e, k, e + 2)
            with act.Fori(NT, NB - 1, 2) as n2:
                for k in range(2):
                    blk(n2 + k, k)
            blk(NB - 1, (NB - 1) % 2, last=True)
            y_out(NB - 1, (NB - 1) % 2)

        @block.vector
        def _(dve):
            v = nc.vector
            chain = [0]

            def link(ins):
                chain[0] += 1
                ins.then_inc(s_ch, 1)
                dve.wait_ge(s_ch, chain[0])

            for k in range(2):
                v.memset(stage[96:P, k, GU_N:HALF], 0.0).then_inc(s_zero, 1)
            v.memset(y[:, 0, :], 0.0).then_inc(s_zero, 1)
            v.memset(h[:, :], 0.0)
            v.memset(eoff[0:1, 0:NT], SHARED * SLOT)
            dve.wait_ge(s_tanh, 1)
            link(v.tensor_scalar(gff[:, :], tanh_g[:, 1:2], YSCALE, None, ALU.mult))
            v.tensor_copy(wcol[:, 0:NT], gff[:, :].broadcast_to([P, NT]))
            dve.wait_ge(s_wrh, 1)
            v.scalar_tensor_tensor(wr16[:, LO].rearrange("p c e -> p (c e)"), wr_sb[:, :, :].rearrange("p c e -> p (c e)"), WSCALE,
                                   wr16[:, HI].rearrange("p c e -> p (c e)"), ALU.mult, ALU.subtract).then_inc(s_wrl, 1)

            def split_lo(n, dst, src, hi):
                dve.wait_ge(s_hi, n + 1)
                v.tensor_tensor(dst, src, hi, ALU.subtract).then_inc(s_lo, 1)

            def logits_out(b, q):
                dve.wait_ge(s_lg, NQ * b + q + 1)
                v.scalar_tensor_tensor(logits[:, bass.ds((b * NQ + q) * E, E)], LG[:, q * E:(q + 1) * E], 1.0 / WSCALE,
                                       br_sb[:, :], ALU.mult, ALU.add).then_inc(s_lgf, 1)

            def step(s2, s1, base):
                number = groups(s2, s1, base)
                if s1 is not None:
                    dve.wait_ge(s_x, 16 * (s1 + 1))
                    for q in range(NQ):
                        v.bn_stats(st1[:, q, :], x_sb[:, rows(s1, q)]).then_inc(s_bn1, 1)
                    need(dve, s_n1, s1)
                    wait_apart(dve, s_bn1, NQ * (s1 + 1))
                    for q in range(NQ):
                        v.bn_aggr(mv1[:, q, :], st1[:, q, :]).then_inc(s_ag1, 1)
                    dve.wait_ge(s_ag1, NQ * (s1 + 1))
                    v.tensor_scalar(ve1[:, :], mv1[:, :, 1], EPS, None, ALU.add)
                    v.tensor_scalar(nm1[:, :], mv1[:, :, 0], -1.0, None, ALU.mult).then_inc(s_v1, 1)
                for q in range(NQ):
                    i = q % 2
                    if s1 is not None:
                        dve.wait_ge(s_eb, 8 * s1 + 5 + q)
                        need(dve, s_ef, 8 * (s1 - 1) + 5 + q)
                        v.reduce_max(negmax[:, q:q + 1], EB[i][:, :], axis=AX_X, negate=True).then_inc(s_max, 1)
                    if s2 is not None:
                        dve.wait_ge(s_xm, NQ * s2 + q + 1)
                        need(dve, s_x2n, NQ * s2 + q - 1)
                        need(dve, s_st_x2[i], 16 * (NQ // 2 * s2 + q // 2))
                        v.scalar_tensor_tensor(x2[:, i, :], XM[i][:, :], tanh_g[:, 0:1], x_sb[:, rows(s2, q)],
                                               ALU.mult, ALU.add).then_inc(s_x2, 1)
                        dve.wait_ge(s_x2, NQ * s2 + q + 1)
                        v.bn_stats(st2[:, i, :], x2[:, i, :]).then_inc(s_bn2, 1)
                        wait_apart(dve, s_bn2, NQ * s2 + q + 1)
                        v.bn_aggr(mv2[:, i, :], st2[:, i, :]).then_inc(s_ag2, 1)
                        dve.wait_ge(s_ag2, NQ * s2 + q + 1)
                        need(dve, s_n2, NQ * s2 + q - 1)
                        v.tensor_scalar(ve2[:, i:i + 1], mv2[:, i, 1:2], EPS, None, ALU.add)
                        v.tensor_scalar(nm2[:, i:i + 1], mv2[:, i, 0:1], -1.0, None, ALU.mult).then_inc(s_v2, 1)
                    if s1 is not None:
                        dve.wait_ge(s_ef, 8 * s1 + 5 + q)
                        need(dve, s_pn, NQ * (s1 - 1) + q + 1)
                        v.reciprocal(rinv[:, q:q + 1], rowsum[:, q:q + 1]).then_inc(s_rec, 1)
                        split_lo(number("xn", q), xnt(s1, LO, q), TP[par("xn", q, s2, s1)][:, :], xnt(s1, HI, q))
                        split_lo(number("p", q), att_cols(s1, LO, q),
                                 TP[par("p", q, s2, s1)][:, :].rearrange("p (c m) -> p c m", c=DC), att_cols(s1, HI, q))
                    if s2 is not None:
                        split_lo(number("x2", q), xT2[:, i, LO, :], TP[par("x2", q, s2, s1)][:, :], xT2[:, i, HI, :])
                        if q > 0:
                            logits_out(s2, q - 1)
                if s2 is not None:
                    logits_out(s2, NQ - 1)

            steps(dve, step)

            def convert(slot, k, u):
                dve.wait_ge(s_cvh, u + 1)
                o = slot * SLOT + k * 2 * HALF
                v.scalar_tensor_tensor(W[:, bass.ds(o + HALF, HALF)], stage[:, k, :], WSCALE, W[:, bass.ds(o, HALF)],
                                       ALU.mult, ALU.subtract).then_inc(s_cvl, 1)

            for k in range(2):
                convert(SHARED, k, k)

            dve.wait_ge(s_lgf, NT)
            dve.wait_ge(s_par, 16 * 9)
            dve.wait_ge(s_const, CONSTS)
            l3 = logits[:, :].rearrange("p (t e) -> p t e", e=E)
            v.tensor_tensor(lrb.rearrange("p (t e) -> p t e", e=E), l3, rb_sb[:, :].unsqueeze(1).broadcast_to([P, NT, E]), ALU.add).then_inc(s_lrb, 1)
            dve.wait_ge(s_ex, 1)
            link(v.tensor_scalar(pr, pr, 1.0, None, ALU.add))
            link(v.reciprocal(pr, pr))
            p3 = pr.rearrange("p (t e) -> p t e", e=E)
            other = p3.unsqueeze(2).broadcast_to([P, NT, E, E])
            own = p3.unsqueeze(3).broadcast_to([P, NT, E, E])
            sq = dict(e=E, f=E)
            b4, t4 = (z.rearrange("p (t e f) -> p t e f", **sq) for z in (beats, ties))
            link(v.tensor_tensor(b4, other, own, ALU.is_gt))
            link(v.tensor_tensor(t4, other, own, ALU.is_equal))
            link(v.tensor_tensor(t4, t4, tri_lt[:, :, :].unsqueeze(1).broadcast_to([P, NT, E, E]), ALU.mult))
            link(v.tensor_tensor(beats, beats, ties, ALU.add))
            link(v.tensor_reduce(rank.rearrange("p (t e) -> p t e", e=E), b4, AX_X, ALU.add))
            v.tensor_scalar(sel16, rank, float(TOPK), None, ALU.is_lt).then_inc(s_sel, 1)
            for k in range(TOPK):
                link(v.tensor_scalar(selk[:, k * TE:(k + 1) * TE], rank, float(k), None, ALU.is_equal))
            s4, d4 = (z.rearrange("p (k n) -> p k n", k=TOPK) for z in (selk, prodk))
            dke = prodk.rearrange("p (i e) -> p i e", e=E)
            link(v.tensor_tensor(d4, s4, pr.unsqueeze(1).broadcast_to([P, TOPK, TE]), ALU.mult))
            link(v.tensor_reduce(topv, dke, AX_X, ALU.add))
            link(v.tensor_tensor(vsum, topv[:, 0:NT], topv[:, NT:KT_N], ALU.add))
            link(v.reciprocal(vinv, vsum))
            wk3 = wk_f.rearrange("p (k t) -> p k t", k=TOPK)
            link(v.tensor_tensor(wk3, topv.rearrange("p (k t) -> p k t", k=TOPK), vinv.unsqueeze(1).broadcast_to([P, TOPK, NT]), ALU.mult))
            link(v.tensor_copy(whi, wk_f))
            link(v.tensor_tensor(wlo, wk_f, whi, ALU.subtract))
            dve.wait_ge(s_pos, 1)
            link(v.tensor_tensor(cgt.rearrange("p (e c) -> p e c", e=E), RB[:, TE:TE + E].unsqueeze(2).broadcast_to([P, E, NT]),
                                 cnt_iota[:, :].unsqueeze(1).broadcast_to([P, E, NT]), ALU.is_gt))
            link(v.tensor_reduce(nblk, cgt.rearrange("p (e c) -> p e c", e=E), AX_X, ALU.add))
            link(v.tensor_tensor(endm.rearrange("p (e f) -> p e f", e=E), tri_le[:, :, :], nblk.unsqueeze(1).broadcast_to([P, E, E]), ALU.mult))
            link(v.tensor_reduce(endb, endm.rearrange("p (e f) -> p e f", e=E), AX_X, ALU.add))
            link(v.tensor_tensor(startb, endb, nblk, ALU.subtract))
            link(v.scalar_tensor_tensor(slot_te.rearrange("p (t e) -> p t e", e=E), startb.unsqueeze(1).broadcast_to([P, NT, E]), float(P),
                                        RB[:, 0:TE].rearrange("p (t e) -> p t e", e=E), ALU.mult, ALU.add))
            link(v.tensor_tensor(d4, s4, slot_te.unsqueeze(1).broadcast_to([P, TOPK, TE]), ALU.mult))
            link(v.tensor_reduce(slotk, dke, AX_X, ALU.add))
            link(v.tensor_copy(slot_i, slotk))
            link(v.tensor_scalar(lane_i, slot_i, P - 1, None, ALU.bitwise_and))
            link(v.tensor_scalar(blk_i, slot_i, P.bit_length() - 1, None, ALU.arith_shift_right))
            link(v.tensor_tensor(lane1h, lane_i.unsqueeze(2).broadcast_to([P, KT_N, P]),
                                 lane_iota[:, :].unsqueeze(1).broadcast_to([P, KT_N, P]), ALU.is_equal))
            link(v.tensor_tensor(blk1h[:, :, 0, :], blk_i.unsqueeze(2).broadcast_to([P, KT_N, NR]),
                                 lane_iota[:, 0:NR].unsqueeze(1).broadcast_to([P, KT_N, NR]), ALU.is_equal))
            for f, z in enumerate((tok_id[:, :], whi, wlo)):
                last = v.tensor_tensor(blk1h[:, :, f + 1, :], blk1h[:, :, 0, :], z.unsqueeze(2).broadcast_to([P, KT_N, NR]), ALU.mult)
            last.then_inc(s_1h, 1)
            link(v.tensor_tensor(eb_m[0:1, :].rearrange("p (n e) -> p n e", e=E), endb[0:1, :].unsqueeze(1).broadcast_to([1, NR, E]),
                                 lane_iota[0:1, 0:NR].unsqueeze(2).broadcast_to([1, NR, E]), ALU.is_le))
            link(v.tensor_reduce(eb_f[0:1, :], eb_m[0:1, :].rearrange("p (n e) -> p n e", e=E), AX_X, ALU.add))
            link(v.tensor_scalar(eoff[0:1, NT:NB], eb_f[0:1, :], float(E - 1), float(SLOT), ALU.min, ALU.mult))
            dve.wait_ge(s_tab, 1)
            occ, tid, th, tl = (RB[:, f * NR:(f + 1) * NR] for f in range(4))
            link(v.tensor_copy(tok[:, NT:NB], tid))
            link(v.tensor_scalar(tgt_f, occ, pad_neg[:, 0:1], pad_row[:, 0:1], ALU.mult, ALU.add))
            link(v.tensor_tensor(tgt[:, NT:NB], tgt_f, tid, ALU.add))
            link(v.tensor_scalar(w_f, th, gff[:, 0:1], None, ALU.mult))
            v.scalar_tensor_tensor(wcol[:, NT:NB], tl, gff[:, 0:1], w_f, ALU.mult, ALU.add).then_inc(s_route, 1)

            def xT_lo(n):
                dve.wait_ge(s_xth, n + 1)
                v.tensor_tensor(xT[:, LO, :], PXT[:, :], xT[:, HI, :], ALU.subtract).then_inc(s_xtl, 1)

            def blk(n, last=False):
                dve.wait_ge(s_silu, n + 1)
                need(dve, s_ht, n)
                v.tensor_tensor(h[:, 0:H], PU[:, 0:H], silu_g[:, :], ALU.mult).then_inc(s_h, 1)
                if not last:
                    xT_lo(n + 1)
                dve.wait_ge(s_hth, n + 1)
                v.tensor_tensor(hT[:, LO, :], PHT[:, 0:HC * P], hT[:, HI, :], ALU.subtract).then_inc(s_htl, 1)

            xT_lo(0)
            for n in range(4):
                blk(n)
                convert(n // 2, n % 2, n + 2)
            with dve.Fori(2, E) as e:
                for k in range(2):
                    blk(2 * e + k)
                    convert(e, k, 2 * e + k + 2)
            with dve.Fori(NT, NB - 1, 2) as n2:
                for k in range(2):
                    blk(n2 + k)
            blk(NB - 1, last=True)

        @block.tensor
        def _(pe):
            t = nc.tensor

            def transposes(bank, src, count, s):
                for c in range(count):
                    last = t.transpose(bank[:, c * P:(c + 1) * P], src(c), ident[:, :])
                last.then_inc(s, 1)

            pe.wait_ge(s_const, CONSTS)
            pe.wait_ge(s_par, 16 * 9)
            transposes(RB, lambda c: wqk[:, c // CC, c % CC * P:(c % CC + 1) * P], 2 * CC, s_wT)
            pe.wait_ge(s_wTc, 1)

            def attend(b, q, base):
                pe.wait_ge(s_lo, base)
                need(pe, s_x2, NQ * b + q - 1)
                bank = XM[q % 2]
                for c in range(DC):
                    chunk = xnt(b, HI, q, c)
                    t.matmul(bank[:, :], chunk, att(b, HI, c), start=(c == 0), stop=False)
                    t.matmul(bank[:, :], chunk, att(b, LO, c), start=False, stop=False)
                    last = t.matmul(bank[:, :], xnt(b, LO, q, c), att(b, HI, c), start=False, stop=(c == DC - 1))
                last.then_inc(s_xm, 1)

            def route_logits(b, q, done):
                pe.wait_ge(s_lo, done + 1)
                need(pe, s_lgf, NQ * b + q)
                dst = LG[:, q * E:(q + 1) * E]
                for c in range(DC):
                    hi, lo = (xT2[:, q % 2, l, c * P:(c + 1) * P] for l in (HI, LO))
                    t.matmul(dst, hi, wr16[:, HI, c, :], start=(c == 0), stop=False)
                    t.matmul(dst, hi, wr16[:, LO, c, :], start=False, stop=False)
                    last = t.matmul(dst, lo, wr16[:, HI, c, :], start=False, stop=(c == DC - 1))
                last.then_inc(s_lg, 1)

            def step(s2, s1, base):
                number = groups(s2, s1, base)
                if s1 is not None:
                    pe.wait_ge(s_ctx, 16 * (s1 + 1))
                    for c in range(CC):
                        need(pe, s_ef, 8 * s1 + c - 1)
                        transposes(EB[c], lambda n: ctx_sb[:, n, c * P:(c + 1) * P], NQ, s_eb)
                if s2 is not None:
                    attend(s2, 0, base)
                if s1 is not None:
                    pe.wait_ge(s_ef, 8 * s1 + CC)
                    for m in range(2):
                        for c in range(CC):
                            last = t.matmul(EB[m][:, :], wqkT[:, m, c, :], ctxT[:, c, :], start=(c == 0), stop=(c == CC - 1))
                        last.then_inc(s_eb, 1)
                for q in range(NQ):
                    i = q % 2
                    if s1 is not None:
                        pe.wait_ge(s_ef, 8 * s1 + max(4, 3 + q))
                        t.matmul(EB[i][:, :], qT[:, q * P:(q + 1) * P], kT, start=True, stop=True).then_inc(s_eb, 1)
                        pe.wait_ge(s_xn, NQ * s1 + q + 1)
                        need(pe, s_lo, number("xn", q) - 1)
                        transposes(TP[par("xn", q, s2, s1)], lambda c: xn[:, i, c * P:(c + 1) * P], DC, s_xnt)
                    if s2 is not None and q < NQ - 1:
                        attend(s2, q + 1, base)
                    if s1 is not None:
                        pe.wait_ge(s_pn, NQ * s1 + q + 1)
                        need(pe, s_lo, number("p", q) - 1)
                        transposes(TP[par("p", q, s2, s1)], lambda c: prob[:, i, c * P:(c + 1) * P], DC, s_pt)
                    if s2 is not None:
                        pe.wait_ge(s_x2n, NQ * s2 + q + 1)
                        need(pe, s_lo, number("x2", q) - 1)
                        transposes(TP[par("x2", q, s2, s1)], lambda c: x2n[:, i, c * P:(c + 1) * P], DC, s_xt2)
                        if q > 0:
                            route_logits(s2, q - 1, number("x2", q - 1))
                if s2 is not None:
                    route_logits(s2, NQ - 1, number("x2", NQ - 1))

            pe.wait_ge(s_wrl, 1)
            steps(pe, step)

            pe.wait_ge(s_sel, 1)
            t.matmul(RB[:, 0:TE], tri16[:, :], sel16, start=True, stop=False, skip_group_check=True)
            for j in range(NT):
                rest = NT - j
                last = t.matmul(RB[:, (j + 1) * E:(NT + 1) * E].rearrange("p (r e) -> p r e", e=E), ones16[:, :],
                                sel16[:, j * E:(j + 1) * E].unsqueeze(1).broadcast_to([P, rest, E]),
                                start=False, stop=(j == NT - 1), skip_group_check=True)
            last.then_inc(s_pos, 1)
            pe.wait_ge(s_1h, 1)
            table = RB[:, 0:4 * NR]
            for i in range(KT_N):
                last = t.matmul(table, lane1h[:, i, :], blk1h[:, i, :, :].rearrange("p f n -> p (f n)"),
                                start=(i == 0), stop=(i == KT_N - 1))
            last.then_inc(s_tab, 1)

            def gate_up(n, off):
                pe.wait_ge(s_xtl, n + 1)
                for c in range(DC):
                    hi, lo = (xT[:, l, c * P:(c + 1) * P] for l in (HI, LO))
                    for m, bank in enumerate((PG, PU)):
                        t.matmul(bank[:, 0:H], hi, gu_w(off, HI, m, c), start=(c == 0), stop=False)
                        t.matmul(bank[:, 0:H], hi, gu_w(off, LO, m, c), start=False, stop=False)
                    for m, bank in enumerate((PG, PU)):
                        last = t.matmul(bank[:, 0:H], lo, gu_w(off, HI, m, c), start=False, stop=(c == DC - 1))
                last.then_inc(s_gu, 1)

            def down(n, off):
                pe.wait_ge(s_htl, n + 1)
                need(pe, s_y, n)
                for j in range(HC):
                    hi, lo = (hT[0:HK[j], l, j * P:(j + 1) * P] for l in (HI, LO))
                    t.matmul(PY[:, :], hi, dn_w(off, HI, j), start=(j == 0), stop=False)
                    t.matmul(PY[:, :], hi, dn_w(off, LO, j), start=False, stop=False)
                    last = t.matmul(PY[:, :], lo, dn_w(off, HI, j), start=False, stop=(j == HC - 1))
                last.then_inc(s_dn, 1)

            def turn_x(n, i, gathered):
                pe.wait_ge(s_xg[i], 16 * gathered)
                transposes(PXT, lambda c: xg[:, i, c * P:(c + 1) * P], DC, s_xt)

            def blk(n, i, half, off, before):
                gate_up(n, off)
                if half is not None:
                    turn_x(n + 1, 1 - i, half + 1 + (i == 1))
                if before is not None:
                    down(n - 1, before)
                pe.wait_ge(s_h, n + 1)
                transposes(PHT, lambda c: h[:, c * P:(c + 1) * P], HC, s_ht)

            def expert(n):
                return pe.value_load(eoff[0:1, bass.ds(n, 1)], min_val=0, max_val=E * SLOT)

            pe.wait_ge(s_lo, GROUPS)
            pe.wait_ge(s_x2, NT)
            pe.wait_ge(s_cvl, 2)
            turn_x(0, 0, 1)
            shared = SHARED * SLOT
            for n in range(4):
                blk(n, n % 2, n // 2, shared, shared if n else None)
            with pe.Fori(2, NT // 2) as r:
                for i in range(2):
                    blk(2 * r + i, i, r, shared, shared)
            pe.wait_ge(s_cvl, 2 + 2 * E)
            with pe.Fori(NT // 2, (NB - 1) // 2) as r:
                for i in range(2):
                    n = 2 * r + i
                    blk(n, i, r, expert(n), expert(n - 1))
            blk(NB - 1, 0, None, expert(NB - 1), expert(NB - 2))
            down(NB - 1, expert(NB - 1))


_INS = ["x", "ctx_1024", "g_xattn", "g_ffn", "L0_xattn_Wq", "L0_xattn_bq", "L0_xattn_Wk", "L0_xattn_bk",
        "L0_ffn_Wg_s", "L0_ffn_Wu_s", "L0_ffn_Wd_s", "L0_ffn_Wg", "L0_ffn_Wu", "L0_ffn_Wd",
        "L0_ffn_Wr", "L0_ffn_br", "L0_ffn_rb"]


def kernel(**inputs):
    import numpy as np
    import concourse.bacc as bacc
    from concourse.bass_utils import run_bass_kernel_spmd

    nc = bacc.Bacc("TRN2", target_bir_lowering=False, num_devices=1)
    arrays, args = {}, []
    for name in _INS:
        a = np.ascontiguousarray(inputs[name])
        arrays[f"in_{name}"] = a
        args.append(nc.dram_tensor(f"in_{name}", a.shape, mybir.dt.from_np(a.dtype), kind="ExternalInput").ap())
    b, s, d = inputs["x"].shape
    out = nc.dram_tensor("out_rows", (b * s + P, d), F32, kind="ExternalOutput").ap()
    flamingo_block(nc, *args, out)
    got = run_bass_kernel_spmd(nc, [arrays], core_ids=[0]).results[0]["out_rows"]
    return got[:b * s].reshape(b, s, d)
```

```python
from contextlib import ExitStack

import concourse.bass as bass
from concourse import mybir

F32 = mybir.dt.float32
F16 = mybir.dt.float16
U32 = mybir.dt.uint32
I32 = mybir.dt.int32
ALU = mybir.AluOpType
ACT = mybir.ActivationFunctionType
AX_X = mybir.AxisListType.X

P = 128
EPS = 1e-5
WSCALE = 64.0
YSCALE = 1.0 / (WSCALE * WSCALE)
HI, LO = 0, 1


def flamingo_block(nc, x, ctx_in, g_x, g_f, wq, bq, wk, bk, wg_s, wu_s, wd_s, wg, wu, wd, wr, br, rb, out):
    B, S, D = x.shape
    C = ctx_in.shape[2]
    E, _, H = wg.shape
    T = B * S
    NQ = S // P
    NT = T // P
    DC = D // P
    CC = C // P
    HC = -(-H // P)
    HK = [min(P, H - P * j) for j in range(HC)]
    TOPK = 2
    NR = (TOPK * T + E * (P - 1)) // P
    NB = NT + NR
    assert (S, D, C, wq.shape[0], DC, NQ) == (512, 512, 256, P, 4, 4) and NT % 2 == 0 and NR % 2 == 1

    GU_N = 2 * (DC // 2) * H
    DN_N = HC * (D // 2)
    HALF = GU_N + DN_N
    SLOT = 4 * HALF
    SHARED = E

    out_t = out[0:T, :].rearrange("(n p) d -> n p d", p=P)
    x_v = x.rearrange("b (q p) d -> b p q d", p=P)
    ctx_v = ctx_in.rearrange("b (q p) c -> b p q c", p=P)
    x2n_rows = nc.dram_tensor("x2n_rows", [T, D], F32).ap()
    x2n_t = x2n_rows.rearrange("(n p) d -> n p d", p=P)

    es = ExitStack()
    with es:
        def sb(name, shape, dt=F32):
            return es.enter_context(nc.sbuf_tensor(name, shape, dt))

        def sem(name):
            return es.enter_context(nc.semaphore(name))

        banks = [es.enter_context(nc.psum_tensor(f"bank{i}", [P, 512], F32)) for i in range(8)]
        EB, TP, XM, LG, RB = banks[0:2], banks[2:4], banks[4:6], banks[6], banks[7]
        TPX, TPP, TPY = TP[0], TP[1], RB
        PG, PU, PXT, PHT, PY = EB[0], EB[1], TP[0], TP[1], XM[0]

        W = sb("W", [P, (E + 1) * SLOT], F16)
        over32 = W[:, 0:E * SLOT].bitcast(F32)
        at = [0]

        def carve(n):
            at[0] += n
            return at[0] - n

        def o32(n):
            o = carve(n)
            return over32[:, o:o + n]

        AT0 = 2 * carve(B * DC * S)
        XNT0 = 2 * carve(B * DC * S)
        ABS = 2 * DC * S
        ctx_sb = o32(NQ * C).rearrange("p (q c) -> p q c", q=NQ)
        ctxT = o32(CC * S).rearrange("p (c n) -> p c n", c=CC)
        qT, kT = o32(S), o32(S)
        prob = o32(2 * S).rearrange("p (i n) -> p i n", i=2)
        xn = o32(2 * D).rearrange("p (i n) -> p i n", i=2)
        x2 = o32(2 * D).rearrange("p (i n) -> p i n", i=2)
        x2n = o32(2 * D).rearrange("p (i n) -> p i n", i=2)
        xT2_0 = 2 * carve(2 * D)
        xT2 = W[:, xT2_0:xT2_0 + 4 * D].rearrange("p (i l n) -> p i l n", i=2, l=2)
        X0 = E * SLOT // 2 - B * NQ * D
        assert at[0] <= X0
        x_sb = over32[:, X0:X0 + B * NQ * D]

        rt = [at[0]]

        def r32(n):
            rt[0] += n
            assert rt[0] <= E * SLOT // 2
            return over32[:, rt[0] - n:rt[0]]

        def r16(n):
            return r32((n + 1) // 2).bitcast(F16)

        TE = NT * E
        KT_N = TOPK * NT
        logits = sb("logits", [P, TE])
        lrb, pr = r32(TE), r32(TE)
        eqv, pr2, best = r32(TE), r32(TE), r32(NT)
        selk, prodk = r32(TOPK * TE), r32(TOPK * TE)
        topv, wk_f = r32(KT_N), r32(KT_N)
        vsum, vinv = r32(NT), r32(NT)
        sel16 = r16(TE)
        whi, wlo = r16(KT_N), r16(KT_N)
        cgt, endm = r32(E * NT), r32(E * E)
        nblk, endb, startb = r32(E), r32(E), r32(E)
        slot_te, slotk = r32(TE), r32(KT_N)
        slot_i, lane_i, blk_i = (r32(KT_N).bitcast(I32) for _ in range(3))
        lane1h = r16(KT_N * P).rearrange("p (i l) -> p i l", l=P)
        blk1h = r16(KT_N * 4 * NR).rearrange("p (i f n) -> p i f n", f=4, n=NR)
        tgt_f, w_f = r32(NR), r32(NR)
        eb_m, eb_f = r32(NR * E), r32(NR)

        tok = sb("tok", [P, NR], U32)
        tgt = sb("tgt", [P, NB], U32)
        wcol = sb("wcol", [P, NB])
        eoff = sb("eoff", [1, NB], I32)

        stage = sb("stage", [P, 2, HALF])
        xg = sb("xg", [P, 2, D])
        xT = sb("xT", [P, 2, D], F16)
        silu_g = sb("silu_g", [P, H])
        h = sb("h", [P, HC * P])
        hT = sb("hT", [P, 2, HC * P], F16)
        y = sb("y", [P, 2, D])
        idx_g = sb("idx_g", [P, 2], U32)
        idx_s = sb("idx_s", [P, 2], U32)

        ident = sb("ident", [P, P])
        ones16 = sb("ones16", [P, P], F16)
        tri16 = sb("tri16", [P, P], F16)
        lane_iota = sb("lane_iota", [P, P])
        cnt_iota = sb("cnt_iota", [P, NT])
        rev_e = sb("rev_e", [P, E])
        tri_le = sb("tri_le", [P, E, E])
        tok_id = sb("tok_id", [P, KT_N])
        pad_row = sb("pad_row", [P, 1])
        pad_neg = sb("pad_neg", [P, 1])
        mhalf = sb("mhalf", [P, NQ])
        wqk = sb("wqk", [P, 2, C])
        wqkT = sb("wqkT", [P, 2, CC, P])
        bqk = sb("bqk", [P, 2])
        gates = sb("gates", [P, 2])
        tanh_g = sb("tanh_g", [P, 2])
        gff = sb("gff", [P, 1])
        br_sb, rb_sb = sb("br_sb", [P, E]), sb("rb_sb", [P, E])
        wr_sb = sb("wr_sb", [P, DC, E])
        wr16 = sb("wr16", [P, 2, DC, E], F16)

        st1, mv1 = sb("st1", [P, NQ, 6]), sb("mv1", [P, NQ, 2])
        ve1, nm1, rstd1, nb1 = (sb(n, [P, NQ]) for n in ("ve1", "nm1", "rstd1", "nb1"))
        st2, mv2 = sb("st2", [P, 2, 6]), sb("mv2", [P, 2, 2])
        ve2, nm2, rstd2, nb2 = (sb(n, [P, 2]) for n in ("ve2", "nm2", "rstd2", "nb2"))
        negmax, rowsum, rinv = (sb(n, [P, NQ]) for n in ("negmax", "rowsum", "rinv"))

        s_const = sem("s_const")
        s_wqk = sem("s_wqk")
        s_par = sem("s_par")
        s_x = sem("s_x")
        s_ctx = sem("s_ctx")
        s_wT, s_wTc = sem("s_wT"), sem("s_wTc")
        s_tanh, s_gff = sem("s_tanh"), sem("s_gff")
        s_wrh, s_wrl = sem("s_wrh"), sem("s_wrl")
        s_eb, s_ef = sem("s_eb"), sem("s_ef")
        s_xnt, s_pt, s_xt2 = sem("s_xnt"), sem("s_pt"), sem("s_xt2")
        s_xnh, s_xnl = sem("s_xnh"), sem("s_xnl")
        s_ph, s_pl = sem("s_ph"), sem("s_pl")
        s_x2h, s_x2l = sem("s_x2h"), sem("s_x2l")
        s_max, s_rec, s_pn = sem("s_max"), sem("s_rec"), sem("s_pn")
        s_bn1, s_ag1, s_v1 = sem("s_bn1"), sem("s_ag1"), sem("s_v1")
        s_bn2, s_ag2, s_v2 = sem("s_bn2"), sem("s_ag2"), sem("s_v2")
        s_pow1, s_n1 = sem("s_pow1"), sem("s_n1")
        s_pow2, s_n2 = sem("s_pow2"), sem("s_n2")
        s_xn, s_x2n = sem("s_xn"), sem("s_x2n")
        s_xm, s_x2 = sem("s_xm"), sem("s_x2")
        s_lg, s_lgf = sem("s_lg"), sem("s_lgf")
        s_st_x2 = [sem("s_st_x2_0"), sem("s_st_x2_1")]
        s_st_n = [sem("s_st_n_0"), sem("s_st_n_1")]
        s_pad = sem("s_pad")
        s_ch = sem("s_ch")
        s_lrb, s_ex = sem("s_lrb"), sem("s_ex")
        s_sel, s_pos, s_1h, s_tab = sem("s_sel"), sem("s_pos"), sem("s_1h"), sem("s_tab")
        s_route = sem("s_route")
        s_stg = [sem("s_stg_0"), sem("s_stg_1")]
        s_shh = sem("s_shh")
        s_cvh, s_cvl = sem("s_cvh"), sem("s_cvl")
        s_zero = sem("s_zero")
        s_idxg, s_idxs = sem("s_idxg"), sem("s_idxs")
        s_xg = [sem("s_xg_0"), sem("s_xg_1")]
        s_xt, s_xth, s_xtl = sem("s_xt"), sem("s_xth"), sem("s_xtl")
        s_gu, s_silu, s_h = sem("s_gu"), sem("s_silu"), sem("s_h")
        s_ht, s_hth, s_htl = sem("s_ht"), sem("s_hth"), sem("s_htl")
        s_apart = sem("s_apart")
        s_dn, s_y = sem("s_dn"), sem("s_y")
        s_sc = sem("s_sc")

        POS_BLOCK, TAB_BLOCK, PEELED = 4, 9, 11
        FIRST_OVER_ROUTE = 4 * at[0] // SLOT

        def halves_at(n):
            return [n - 1] if n < 2 else [1, 2] if n == 2 else [n] if n < PEELED - 1 else [n, n + 1]

        assert sum(map(len, map(halves_at, range(1, PEELED)))) + NT - 1 - PEELED == 2 * E
        assert all(u < FIRST_OVER_ROUTE for n in range(1, TAB_BLOCK) for u in halves_at(n))

        block = es.enter_context(nc.Block())

        def need(eng, s, v):
            if not isinstance(v, int) or v > 0:
                eng.wait_ge(s, v)

        CONSTS, PARS = 14, 7

        def wait_apart(eng, s, v):
            eng.wait_ge(s, v)
            eng.sem_inc(s_apart, 1)

        def two_before(eng, s, b, q):
            if q > 1:
                eng.wait_ge(s, NQ * b + q - 1)

        def one_before(eng, s, b, q):
            if q > 0:
                eng.wait_ge(s, NQ * b + q)

        def stored_before(eng, s, b, q):
            if q > 1:
                eng.wait_ge(s[q % 2], 16 * (NQ // 2 * b + q // 2))

        def all_stored(eng, s, b):
            for i in range(2):
                eng.wait_ge(s[i], 16 * (NQ // 2) * (b + 1))

        def rows(b, q):
            return bass.ds(b * (NQ * D) + q * D, D)

        def xnt(b, hl, q, c=None):
            o = XNT0 + b * ABS + (hl * DC * S + q * D)
            return W[:, bass.ds(o, D)] if c is None else W[:, bass.ds(o + c * P, P)]

        def att(b, hl, c):
            return W[:, bass.ds(AT0 + b * ABS + (hl * DC * S + c * S), S)]

        def att_cols(b, hl, q):
            whole = W[:, bass.ds(AT0 + b * ABS + hl * DC * S, DC * S)]
            return whole.rearrange("p (c m) -> p c m", c=DC)[:, :, q * P:(q + 1) * P]

        def gu_w(off, hl, m, c):
            k, c2 = divmod(c, DC // 2)
            return W[:, bass.ds(off + (k * 2 * HALF + hl * HALF + (m * (DC // 2) + c2) * H), H)]

        def dn_w(off, hl, j):
            whole = W[:, bass.ds(off, SLOT)].rearrange("p (k r) -> p k r", k=2)
            o = hl * HALF + GU_N + j * (D // 2)
            return whole[0:HK[j], :, o:o + D // 2]

        wg_rows, wu_rows, wd_rows = (w.rearrange("e d n -> (e d) n") for w in (wg, wu, wd))

        @block.sync
        def _(sp):
            def stage_half(k, gate, up, down):
                half = stage[:, k, 0:GU_N].rearrange("p (m c n) -> p m c n", m=2, c=DC // 2)
                rest = stage[:, k, GU_N:HALF].rearrange("p (j n) -> p j n", j=HC)
                sp.dma_start(half[:, 0], gate.rearrange("(c p) n -> p c n", p=P)).then_inc(s_stg[k], 16)
                sp.dma_start(half[:, 1], up.rearrange("(c p) n -> p c n", p=P)).then_inc(s_stg[k], 16)
                sp.dma_start(rest[:, 0:HC - 1], down[0].rearrange("(j p) n -> p j n", p=P)).then_inc(s_stg[k], 16)
                sp.dma_start(rest[0:HK[-1], HC - 1], down[1]).then_inc(s_stg[k], 16)

            def load_ctx(b):
                need(sp, s_eb, 8 * (b - 1) + CC)
                sp.dma_start(ctx_sb, ctx_v[b]).then_inc(s_ctx, 16)

            def load_x(b):
                need(sp, s_x, 16 * b)
                sp.dma_start(x_sb[:, b * NQ * D:(b + 1) * NQ * D].rearrange("p (q d) -> p q d", q=NQ),
                             x_v[b]).then_inc(s_x, 16)

            def store(b):
                for q in range(NQ):
                    i = q % 2
                    tile = bass.ds(b * S + q * P, P)
                    sp.wait_ge(s_x2, NQ * b + q + 1)
                    sp.dma_start(out[tile, :], x2[:, i, :]).then_inc(s_st_x2[i], 16)
                    sp.wait_ge(s_x2n, NQ * b + q + 1)
                    sp.dma_start(x2n_rows[tile, :], x2n[:, i, :]).then_inc(s_st_n[i], 16)

            load_ctx(0)
            sp.wait_ge(s_ctx, 16)
            load_x(0)
            load_x(1)
            sp.wait_ge(s_zero, 3)
            for k in range(2):
                rows_k = slice(k * (D // 2), (k + 1) * (D // 2))
                stage_half(k, wg_s[rows_k, :], wu_s[rows_k, :],
                           (wd_s[0:(HC - 1) * P, rows_k], wd_s[(HC - 1) * P:H, rows_k]))
            load_ctx(1)
            load_x(2)
            load_x(3)
            sp.dma_start(out[T:T + P, :], y[:, 0, :]).then_inc(s_pad, 16)
            for b in range(2):
                load_ctx(b + 2)
                store(b)
            with sp.Fori(2, B) as b:
                store(b)
            with sp.Fori(0, E) as e:
                for k in range(2):
                    sp.wait_ge(s_cvl, 2 * e + k + 1)
                    cols = slice(k * (D // 2), (k + 1) * (D // 2))
                    rows_k = bass.ds(e * D + k * (D // 2), D // 2)
                    stage_half(k, wg_rows[rows_k, :], wu_rows[rows_k, :],
                               (wd_rows[bass.ds(e * H, (HC - 1) * P), cols],
                                wd_rows[bass.ds(e * H + (HC - 1) * P, HK[-1]), cols]))
            sp.wait_ge(s_pad, 16)
            sp.wait_ge(s_sc, 16 * NB)

        @block.gpsimd
        def _(pool):
            g = nc.gpsimd
            iota = dict(allow_small_or_imprecise_dtypes=True)
            g.memset(ident[:, :], 0.0).then_inc(s_const, 1)
            g.memset(ones16[:, :], 1.0).then_inc(s_const, 1)
            g.memset(mhalf[:, :], -0.5).then_inc(s_const, 1)
            g.memset(tri_le[:, :, :], 1.0).then_inc(s_const, 1)
            g.iota(lane_iota[:, :], [[1, P]], base=0, channel_multiplier=0, **iota).then_inc(s_const, 1)
            g.iota(cnt_iota[:, :], [[P, NT]], base=0, channel_multiplier=0, **iota).then_inc(s_const, 1)
            g.iota(tok_id[:, :], [[0, TOPK], [P, NT]], base=0, channel_multiplier=1, **iota).then_inc(s_const, 1)
            g.iota(rev_e[:, :], [[-1, E]], base=E, channel_multiplier=0, **iota).then_inc(s_const, 1)
            g.iota(pad_row[:, :], [[0, 1]], base=T, channel_multiplier=1, **iota).then_inc(s_const, 1)
            g.iota(pad_neg[:, :], [[0, 1]], base=-T, channel_multiplier=-1, **iota).then_inc(s_const, 1)
            g.iota(tgt[:, 0:NT], [[P, NT]], base=0, channel_multiplier=1).then_inc(s_const, 1)
            pool.wait_ge(s_const, 11)
            g.affine_select(out=ident[:, :], in_=ident[:, :], compare_op=ALU.not_equal, fill=1.0,
                            base=0, pattern=[[-1, P]], channel_multiplier=1).then_inc(s_const, 1)
            g.affine_select(out=tri16[:, :], in_=ones16[:, :], compare_op=ALU.is_gt, fill=0.0,
                            base=0, pattern=[[1, P]], channel_multiplier=-1).then_inc(s_const, 1)
            g.affine_select(out=tri_le[:, :, :], in_=tri_le[:, :, :], compare_op=ALU.is_ge, fill=0.0,
                            base=0, pattern=[[1, E], [-1, E]], channel_multiplier=0).then_inc(s_const, 1)
            pool.wait_ge(s_const, CONSTS)

            def scale_x(b):
                pool.wait_ge(s_v1, b + 1)
                need(pool, s_xn, NQ * b)
                g.tensor_tensor(rstd1[:, :], ve1[:, :], mhalf[:, :], ALU.pow).then_inc(s_pow1, 1)
                pool.wait_ge(s_pow1, b + 1)
                g.tensor_tensor(nb1[:, :], nm1[:, :], rstd1[:, :], ALU.mult).then_inc(s_n1, 1)

            def scale_x2(b, q):
                i = slice(q % 2, q % 2 + 1)
                pool.wait_ge(s_v2, NQ * b + q + 1)
                two_before(pool, s_x2n, b, q)
                g.tensor_tensor(rstd2[:, i], ve2[:, i], mhalf[:, 0:1], ALU.pow).then_inc(s_pow2, 1)
                pool.wait_ge(s_pow2, NQ * b + q + 1)
                g.tensor_tensor(nb2[:, i], nm2[:, i], rstd2[:, i], ALU.mult).then_inc(s_n2, 1)

            def step(s2, nx):
                if s2 is not None:
                    for q in range(NQ):
                        scale_x2(s2, q)
                if nx is not None:
                    scale_x(nx)

            def load_tile(n, i):
                need(pool, s_xt, n - 1)
                pool.sem_inc(s_apart, 1)
                g.dma_start(xg[:, i, :], x2n_rows[bass.ds(n * P, P), :]).then_inc(s_xg[i], 16)

            def gather(n, i):
                need(pool, s_xt, n - 1)
                g.tensor_copy(idx_g[:, i:i + 1], tok[:, bass.ds(n - NT, 1)]).then_inc(s_idxg, 1)
                wait_apart(pool, s_idxg, n - NT + 1)
                g.indirect_dma_start(xg[:, i, :], None, x2n_rows,
                                     bass.IndirectOffsetOnAxis(ap=idx_g[:, i:i + 1], axis=0)).then_inc(s_xg[i], 16)

            def scatter(n, i):
                g.tensor_copy(idx_s[:, i:i + 1], tgt[:, bass.ds(n, 1)]).then_inc(s_idxs, 1)
                pool.wait_ge(s_idxs, n + 1)
                need(pool, s_sc, 16 * n)
                wait_apart(pool, s_y, n + 1)
                g.indirect_dma_start(out, bass.IndirectOffsetOnAxis(ap=idx_s[:, i:i + 1], axis=0), y[:, i, :],
                                     None, compute_op=ALU.add).then_inc(s_sc, 16)

            scale_x(0)
            for k in range(2):
                pool.wait_ge(s_stg[k], 64)
                o = SHARED * SLOT + k * 2 * HALF
                g.tensor_scalar(W[:, o:o + HALF], stage[:, k, :], WSCALE, None, ALU.mult).then_inc(s_shh, 1)
            step(None, 1)
            with pool.Fori(0, B - 2) as b:
                step(b, b + 2)
            LEAD = 4
            for i in range(2):
                pool.wait_ge(s_st_n[i], 16 * (LEAD // 2))
            for n in range(2):
                load_tile(n, n % 2)
            step(B - 2, None)
            for n in range(2, LEAD):
                load_tile(n, n % 2)
            step(B - 1, None)
            for i in range(2):
                pool.wait_ge(s_st_n[i], 16 * NT // 2)
                pool.wait_ge(s_st_x2[i], 16 * NT // 2)
            pool.wait_ge(s_pad, 16)
            for n in range(2):
                scatter(n, n % 2)
                load_tile(n + LEAD, n % 2)
            with pool.Fori(1, (NT - LEAD) // 2) as r:
                for i in range(2):
                    scatter(2 * r + i, i)
                    load_tile(2 * r + i + LEAD, i)
            pool.wait_ge(s_route, 1)
            with pool.Fori(NT - LEAD, NB - LEAD - 1, 2) as n2:
                for i in range(2):
                    scatter(n2 + i, i)
                    gather(n2 + i + LEAD, i)
            for n in range(NB - LEAD - 1, NB):
                scatter(n, n % 2)
                if n + LEAD < NB:
                    gather(n + LEAD, n % 2)

        @block.scalar
        def _(act):
            a = nc.scalar
            for dst, src in ((wqk[:, 0, :], wq), (wqk[:, 1, :], wk),
                             (bqk[:, 0:1], bq.rearrange("(p a) -> p a", a=1)), (bqk[:, 1:2], bk.rearrange("(p a) -> p a", a=1)),
                             (gates[:, 0:1], g_x.partition_broadcast(P)), (gates[:, 1:2], g_f.partition_broadcast(P)),
                             (br_sb[:, :], br.partition_broadcast(P)), (rb_sb[:, :], rb.partition_broadcast(P)),
                             (wr_sb[:, :, :], wr.rearrange("(c p) e -> p c e", p=P))):
                act.dma_start(dst, src).then_inc(s_wqk if src in (wq, wk) else s_par, 16)
            act.wait_ge(s_wT, 1)
            a.activation(wqkT[:, :, :, :].rearrange("p a c d -> p (a c d)"), RB[:, 0:2 * C], ACT.Copy).then_inc(s_wTc, 1)

            def context(b, c):
                act.wait_ge(s_eb, 8 * b + c + 1)
                a.activation(ctxT[:, c, :], EB[c][:, :], ACT.Copy).then_inc(s_ef, 1)

            def project(b, m):
                act.wait_ge(s_eb, 8 * b + CC + m + 1)
                a.activation((qT, kT)[m], EB[m][:, :], ACT.Identity, bias=bqk[:, m:m + 1]).then_inc(s_ef, 1)

            def normalise(b, q):
                if q == 0:
                    act.wait_ge(s_n1, b + 1)
                need(act, s_xnt, NQ * b + q - 1)
                a.activation(xn[:, q % 2, :], x_sb[:, rows(b, q)], ACT.Identity, bias=nb1[:, q:q + 1],
                             scale=rstd1[:, q:q + 1]).then_inc(s_xn, 1)

            def xn_hi(b, q):
                act.wait_ge(s_xnt, NQ * b + q + 1)
                a.activation(xnt(b, HI, q), TPX[:, :], ACT.Copy).then_inc(s_xnh, 1)

            def exponentials(b, q):
                act.wait_ge(s_max, NQ * b + q + 1)
                need(act, s_pt, NQ * b + q - 1)
                a.activation(prob[:, q % 2, :], EB[q % 2][:, :], ACT.Exp, bias=negmax[:, q:q + 1],
                             accum_out=rowsum[:, q:q + 1]).then_inc(s_ef, 1)

            def scale_probs(b, q):
                act.wait_ge(s_rec, NQ * b + q + 1)
                a.activation(prob[:, q % 2, :], prob[:, q % 2, :], ACT.Copy, scale=rinv[:, q:q + 1]).then_inc(s_pn, 1)

            def probs_hi(b, q):
                act.wait_ge(s_pt, NQ * b + q + 1)
                a.activation(att_cols(b, HI, q), TPP[:, :].rearrange("p (c m) -> p c m", c=DC), ACT.Copy).then_inc(s_ph, 1)

            def normalise_x2(b, q):
                i = q % 2
                act.wait_ge(s_n2, NQ * b + q + 1)
                two_before(act, s_xt2, b, q)
                stored_before(act, s_st_n, b, q)
                a.activation(x2n[:, i, :], x2[:, i, :], ACT.Identity, bias=nb2[:, i:i + 1],
                             scale=rstd2[:, i:i + 1]).then_inc(s_x2n, 1)

            def x2_hi(b, q):
                act.wait_ge(s_xt2, NQ * b + q + 1)
                two_before(act, s_lg, b, q)
                a.activation(xT2[:, q % 2, HI, :], TPY[:, :], ACT.Copy).then_inc(s_x2h, 1)

            def step(s2, s1, nx):
                for q in range(NQ):
                    if s1 is not None:
                        xn_hi(s1, q)
                        exponentials(s1, q)
                        if q < NQ - 1:
                            normalise(s1, q + 1)
                        if q > 0:
                            probs_hi(s1, q - 1)
                        scale_probs(s1, q)
                    elif q == 1:
                        hT_hi(0)
                    if s2 is not None and q > 0:
                        normalise_x2(s2, q - 1)
                    if s2 is not None and q > 1:
                        x2_hi(s2, q - 2)
                if nx is not None:
                    for c in range(CC):
                        context(nx, c)
                elif s1 is not None:
                    xT_hi(0)
                if s2 is not None:
                    x2_hi(s2, NQ - 2)
                if s1 is not None:
                    probs_hi(s1, NQ - 1)
                if s2 is not None:
                    normalise_x2(s2, NQ - 1)
                if nx is not None:
                    project(nx, 0)
                if s2 is not None:
                    x2_hi(s2, NQ - 1)
                if nx is not None:
                    normalise(nx, 0)
                    project(nx, 1)
                else:
                    n = 0 if s1 is not None else 1
                    silu(n)
                    xT_hi(n + 1)
                if s2 is not None and s1 is not None:
                    all_stored(act, s_st_n, s2)

            def convert(slot, k, loads):
                act.wait_ge(s_stg[k], 64 * loads)
                dst = W[:, bass.ds(slot * SLOT + k * 2 * HALF, HALF)]
                a.activation(dst, stage[:, k, :], ACT.Copy, scale=WSCALE).then_inc(s_cvh, 1)

            def xT_hi(n):
                act.wait_ge(s_xt, n + 1)
                a.activation(xT[:, HI, :], PXT[:, :], ACT.Copy).then_inc(s_xth, 1)

            def y_out(n, i):
                act.wait_ge(s_dn, n + 1)
                need(act, s_sc, 16 * (n - 1))
                a.activation(y[:, i, :], PY[:, :], ACT.Copy, scale=wcol[:, bass.ds(n, 1)]).then_inc(s_y, 1)

            def silu(n):
                act.wait_ge(s_gu, n + 1)
                need(act, s_h, n)
                a.activation(silu_g[:, :], PG[:, 0:H], ACT.Silu, scale=1.0 / WSCALE).then_inc(s_silu, 1)

            def hT_hi(n):
                act.wait_ge(s_ht, n + 1)
                a.activation(hT[:, HI, :], PHT[:, 0:HC * P], ACT.Copy).then_inc(s_hth, 1)

            def blk(n, i, last=False):
                silu(n)
                if not last:
                    xT_hi(n + 1)
                y_out(n - 1, 1 - i)
                hT_hi(n)

            def routed_halves(n):
                for u in halves_at(n):
                    if u == 0:
                        act.wait_ge(s_lgf, B)
                    if u == FIRST_OVER_ROUTE:
                        act.wait_ge(s_route, 1)
                        all_stored(act, s_st_x2, B - 1)
                        all_stored(act, s_st_n, B - 1)
                    convert(u // 2, u % 2, u // 2 + 2)

            for c in range(CC):
                context(0, c)
            act.wait_ge(s_par, 16 * PARS)
            project(0, 0)
            project(0, 1)
            normalise(0, 0)
            a.activation(tanh_g[:, :], gates[:, :], ACT.Tanh).then_inc(s_tanh, 1)
            a.activation(wr16[:, HI], wr_sb[:, :, :], ACT.Copy, scale=WSCALE).then_inc(s_wrh, 1)
            step(None, 0, 1)
            with act.Fori(0, B - 2) as b:
                step(b, b + 1, b + 2)
            step(B - 2, B - 1, None)
            step(B - 1, None, None)

            act.wait_ge(s_pad, 16)
            y_out(0, 0)
            hT_hi(1)
            act.wait_ge(s_lrb, 1)
            a.activation(pr, lrb, ACT.Exp, scale=-1.0).then_inc(s_ex, 1)
            routed_halves(1)
            for n in range(2, PEELED):
                blk(n, n % 2)
                routed_halves(n)
            with act.Fori(PEELED // 2, NT // 2 - 1) as r:
                for k in range(2):
                    blk(2 * r + 1 + k, 1 - k)
                    convert(r + 1, k, r + 3)
            with act.Fori(NT // 2 - 1, (NB - 3) // 2) as r:
                for k in range(2):
                    blk(2 * r + 1 + k, 1 - k)
            blk(NB - 2, (NB - 2) % 2)
            blk(NB - 1, (NB - 1) % 2, last=True)
            y_out(NB - 1, (NB - 1) % 2)

        @block.vector
        def _(dve):
            v = nc.vector
            chain = [0]

            def link(ins):
                chain[0] += 1
                ins.then_inc(s_ch, 1)
                dve.wait_ge(s_ch, chain[0])

            for k in range(2):
                v.memset(stage[96:P, k, GU_N:HALF], 0.0).then_inc(s_zero, 1)
            v.memset(y[:, 0, :], 0.0).then_inc(s_zero, 1)
            v.memset(h[:, :], 0.0)
            v.memset(eoff[0:1, 0:NT], SHARED * SLOT)

            def parameters():
                dve.wait_ge(s_tanh, 1)
                link(v.tensor_scalar(gff[:, :], tanh_g[:, 1:2], YSCALE, None, ALU.mult))
                v.tensor_copy(wcol[:, 0:NT], gff[:, :].broadcast_to([P, NT]))
                dve.wait_ge(s_wrh, 1)
                v.scalar_tensor_tensor(wr16[:, LO].rearrange("p c e -> p (c e)"), wr_sb[:, :, :].rearrange("p c e -> p (c e)"), WSCALE,
                                       wr16[:, HI].rearrange("p c e -> p (c e)"), ALU.mult, ALU.subtract).then_inc(s_wrl, 1)

            def logits_out(b):
                dve.wait_ge(s_lg, NQ * (b + 1))
                to = logits[:, bass.ds(b * NQ * E, NQ * E)].rearrange("p (q e) -> p q e", e=E)
                v.scalar_tensor_tensor(to, LG[:, 0:NQ * E].rearrange("p (q e) -> p q e", e=E), 1.0 / WSCALE,
                                       br_sb[:, :].unsqueeze(1).broadcast_to([P, NQ, E]), ALU.mult, ALU.add).then_inc(s_lgf, 1)

            def x_stats(b, q):
                if q == 0:
                    dve.wait_ge(s_x, 16 * (b + 1))
                v.bn_stats(st1[:, q, :], x_sb[:, rows(b, q)]).then_inc(s_bn1, 1)

            def x_moments(b):
                need(dve, s_n1, b)
                wait_apart(dve, s_bn1, NQ * (b + 1))
                for q in range(NQ):
                    v.bn_aggr(mv1[:, q, :], st1[:, q, :]).then_inc(s_ag1, 1)
                dve.wait_ge(s_ag1, NQ * (b + 1))
                v.tensor_scalar(ve1[:, :], mv1[:, :, 1], EPS, None, ALU.add)
                v.tensor_scalar(nm1[:, :], mv1[:, :, 0], -1.0, None, ALU.mult).then_inc(s_v1, 1)

            def row_max(b, q):
                dve.wait_ge(s_eb, 8 * b + 5 + q)
                need(dve, s_ef, 8 * (b - 1) + 5 + q)
                v.reduce_max(negmax[:, q:q + 1], EB[q % 2][:, :], axis=AX_X, negate=True).then_inc(s_max, 1)

            def row_rec(b, q):
                dve.wait_ge(s_ef, 8 * b + 5 + q)
                need(dve, s_pn, NQ * (b - 1) + q + 1)
                v.reciprocal(rinv[:, q:q + 1], rowsum[:, q:q + 1]).then_inc(s_rec, 1)

            def xn_lo(b, q):
                dve.wait_ge(s_xnh, NQ * b + q + 1)
                v.tensor_tensor(xnt(b, LO, q), TPX[:, :], xnt(b, HI, q), ALU.subtract).then_inc(s_xnl, 1)

            def probs_lo(b, q):
                dve.wait_ge(s_ph, NQ * b + q + 1)
                v.tensor_tensor(att_cols(b, LO, q), TPP[:, :].rearrange("p (c m) -> p c m", c=DC), att_cols(b, HI, q),
                                ALU.subtract).then_inc(s_pl, 1)

            def x2_lo(b, q):
                dve.wait_ge(s_x2h, NQ * b + q + 1)
                v.tensor_tensor(xT2[:, q % 2, LO, :], TPY[:, :], xT2[:, q % 2, HI, :], ALU.subtract).then_inc(s_x2l, 1)

            def add_attention(b, q):
                i = q % 2
                dve.wait_ge(s_xm, NQ * b + q + 1)
                two_before(dve, s_x2n, b, q)
                stored_before(dve, s_st_x2, b, q)
                v.scalar_tensor_tensor(x2[:, i, :], XM[i][:, :], tanh_g[:, 0:1], x_sb[:, rows(b, q)],
                                       ALU.mult, ALU.add).then_inc(s_x2, 1)
                dve.wait_ge(s_x2, NQ * b + q + 1)
                v.bn_stats(st2[:, i, :], x2[:, i, :]).then_inc(s_bn2, 1)

            def x2_moments(b, q):
                i = q % 2
                wait_apart(dve, s_bn2, NQ * b + q + 1)
                v.bn_aggr(mv2[:, i, :], st2[:, i, :]).then_inc(s_ag2, 1)
                two_before(dve, s_n2, b, q)
                dve.wait_ge(s_ag2, NQ * b + q + 1)
                v.tensor_scalar(ve2[:, i:i + 1], mv2[:, i, 1:2], EPS, None, ALU.add)
                v.tensor_scalar(nm2[:, i:i + 1], mv2[:, i, 0:1], -1.0, None, ALU.mult).then_inc(s_v2, 1)

            def step(s2, s1, nx):
                for q in range(NQ):
                    if s1 is not None:
                        row_max(s1, q)
                    if s2 is not None and q > 0:
                        x2_moments(s2, q - 1)
                    if s1 is None and q == 1:
                        hT_lo(0)
                    if s2 is not None and q > 2:
                        x2_lo(s2, q - 3)
                    if s1 is not None:
                        xn_lo(s1, q)
                        row_rec(s1, q)
                    if nx is not None:
                        x_stats(nx, q)
                    if s1 is not None and q > 0:
                        probs_lo(s1, q - 1)
                    if s2 is not None:
                        add_attention(s2, q)
                if s2 is not None:
                    x2_lo(s2, NQ - 3)
                if nx is None and s1 is not None:
                    xT_lo(0)
                if s2 is not None:
                    x2_moments(s2, NQ - 1)
                    x2_lo(s2, NQ - 2)
                if s1 is not None:
                    probs_lo(s1, NQ - 1)
                if nx is not None:
                    x_moments(nx)
                if s2 is not None:
                    x2_lo(s2, NQ - 1)
                if nx is None:
                    n = 0 if s1 is not None else 1
                    gated(n)
                    xT_lo(n + 1)
                if s2 is not None:
                    logits_out(s2)
                    if s1 is not None:
                        all_stored(dve, s_st_x2, s2)

            def convert(slot, k, s_high, u):
                dve.wait_ge(s_high, u + 1)
                o = slot * SLOT + k * 2 * HALF
                v.scalar_tensor_tensor(W[:, bass.ds(o + HALF, HALF)], stage[:, k, :], WSCALE, W[:, bass.ds(o, HALF)],
                                       ALU.mult, ALU.subtract).then_inc(s_cvl, 1)

            l3 = logits[:, :].rearrange("p (t e) -> p t e", e=E)
            lanes = lambda z: z.rearrange("p (t e) -> p t e", e=E)
            by_expert = rev_e[:, :].unsqueeze(1).broadcast_to([P, NT, E])
            s4, d4 = (z.rearrange("p (k n) -> p k n", k=TOPK) for z in (selk, prodk))
            dke = prodk.rearrange("p (i e) -> p i e", e=E)

            def biased_logits():
                dve.wait_ge(s_lgf, B)
                dve.wait_ge(s_const, CONSTS)
                v.tensor_tensor(lanes(lrb), l3, rb_sb[:, :].unsqueeze(1).broadcast_to([P, NT, E]), ALU.add).then_inc(s_lrb, 1)

            def probabilities():
                dve.wait_ge(s_ex, 1)
                link(v.tensor_scalar(pr, pr, 1.0, None, ALU.add))
                link(v.reciprocal(pr, pr))

            def choose(k):
                left = (pr, pr2)[k]
                top, one = topv[:, k * NT:(k + 1) * NT], selk[:, k * TE:(k + 1) * TE]
                link(v.tensor_reduce(top, lanes(left), AX_X, ALU.max))
                link(v.tensor_tensor(lanes(eqv), lanes(left), top.unsqueeze(2).broadcast_to([P, NT, E]), ALU.is_equal))
                link(v.tensor_tensor(lanes(eqv), lanes(eqv), by_expert, ALU.mult))
                link(v.tensor_reduce(best, lanes(eqv), AX_X, ALU.max))
                link(v.tensor_tensor(lanes(one), by_expert, best.unsqueeze(2).broadcast_to([P, NT, E]), ALU.is_equal))
                if k == 0:
                    link(v.scalar_tensor_tensor(pr2, one, -2.0, pr, ALU.mult, ALU.add))
                else:
                    v.tensor_tensor(sel16, selk[:, 0:TE], one, ALU.add).then_inc(s_sel, 1)

            def gate_weights():
                link(v.tensor_tensor(vsum, topv[:, 0:NT], topv[:, NT:KT_N], ALU.add))
                link(v.reciprocal(vinv, vsum))
                wk3 = wk_f.rearrange("p (k t) -> p k t", k=TOPK)
                link(v.tensor_tensor(wk3, topv.rearrange("p (k t) -> p k t", k=TOPK), vinv.unsqueeze(1).broadcast_to([P, TOPK, NT]), ALU.mult))
                link(v.tensor_copy(whi, wk_f))
                link(v.tensor_tensor(wlo, wk_f, whi, ALU.subtract))

            def slots():
                dve.wait_ge(s_pos, 1)
                link(v.tensor_tensor(cgt.rearrange("p (e c) -> p e c", e=E), RB[:, TE:TE + E].unsqueeze(2).broadcast_to([P, E, NT]),
                                     cnt_iota[:, :].unsqueeze(1).broadcast_to([P, E, NT]), ALU.is_gt))
                link(v.tensor_reduce(nblk, cgt.rearrange("p (e c) -> p e c", e=E), AX_X, ALU.add))
                link(v.tensor_tensor(endm.rearrange("p (e f) -> p e f", e=E), tri_le[:, :, :], nblk.unsqueeze(1).broadcast_to([P, E, E]), ALU.mult))
                link(v.tensor_reduce(endb, endm.rearrange("p (e f) -> p e f", e=E), AX_X, ALU.add))
                link(v.tensor_tensor(startb, endb, nblk, ALU.subtract))
                link(v.scalar_tensor_tensor(lanes(slot_te), startb.unsqueeze(1).broadcast_to([P, NT, E]), float(P),
                                            lanes(RB[:, 0:TE]), ALU.mult, ALU.add))
                link(v.tensor_tensor(d4, s4, slot_te.unsqueeze(1).broadcast_to([P, TOPK, TE]), ALU.mult))
                link(v.tensor_reduce(slotk, dke, AX_X, ALU.add))
                link(v.tensor_copy(slot_i, slotk))
                link(v.tensor_scalar(lane_i, slot_i, P - 1, None, ALU.bitwise_and))
                link(v.tensor_scalar(blk_i, slot_i, P.bit_length() - 1, None, ALU.arith_shift_right))

            def lane_onehots(k):
                own = slice(k * NT, (k + 1) * NT)
                link(v.tensor_tensor(lane1h[:, own, :], lane_i[:, own].unsqueeze(2).broadcast_to([P, NT, P]),
                                     lane_iota[:, :].unsqueeze(1).broadcast_to([P, NT, P]), ALU.is_equal))

            def block_field(f):
                if f == 0:
                    link(v.tensor_tensor(blk1h[:, :, 0, :], blk_i.unsqueeze(2).broadcast_to([P, KT_N, NR]),
                                         lane_iota[:, 0:NR].unsqueeze(1).broadcast_to([P, KT_N, NR]), ALU.is_equal))
                else:
                    z = (tok_id[:, :], whi, wlo)[f - 1]
                    last = v.tensor_tensor(blk1h[:, :, f, :], blk1h[:, :, 0, :], z.unsqueeze(2).broadcast_to([P, KT_N, NR]), ALU.mult)
                    if f == 3:
                        last.then_inc(s_1h, 1)

            def block_experts():
                link(v.tensor_tensor(lanes(eb_m[0:1, :]), endb[0:1, :].unsqueeze(1).broadcast_to([1, NR, E]),
                                     lane_iota[0:1, 0:NR].unsqueeze(2).broadcast_to([1, NR, E]), ALU.is_le))
                link(v.tensor_reduce(eb_f[0:1, :], lanes(eb_m[0:1, :]), AX_X, ALU.add))
                link(v.tensor_scalar(eoff[0:1, NT:NB], eb_f[0:1, :], float(E - 1), float(SLOT), ALU.min, ALU.mult))

            def tables():
                dve.wait_ge(s_tab, 1)
                occ, tid, th, tl = (RB[:, f * NR:(f + 1) * NR] for f in range(4))
                link(v.tensor_copy(tok[:, :], tid))
                link(v.tensor_scalar(tgt_f, occ, pad_neg[:, 0:1], pad_row[:, 0:1], ALU.mult, ALU.add))
                link(v.tensor_tensor(tgt[:, NT:NB], tgt_f, tid, ALU.add))
                link(v.tensor_scalar(w_f, th, gff[:, 0:1], None, ALU.mult))
                v.scalar_tensor_tensor(wcol[:, NT:NB], tl, gff[:, 0:1], w_f, ALU.mult, ALU.add).then_inc(s_route, 1)

            def routing_at(n):
                if n == 1:
                    probabilities()
                elif n == 2:
                    choose(0)
                elif n == 3:
                    choose(1)
                    gate_weights()
                elif n == POS_BLOCK:
                    slots()
                elif n <= 6:
                    lane_onehots(n - 5)
                elif n <= 8:
                    block_field(2 * (n - 7))
                    block_field(2 * (n - 7) + 1)
                elif n == TAB_BLOCK:
                    block_experts()
                    tables()

            def xT_lo(n):
                dve.wait_ge(s_xth, n + 1)
                v.tensor_tensor(xT[:, LO, :], PXT[:, :], xT[:, HI, :], ALU.subtract).then_inc(s_xtl, 1)

            def gated(n):
                dve.wait_ge(s_silu, n + 1)
                need(dve, s_ht, n)
                v.tensor_tensor(h[:, 0:H], PU[:, 0:H], silu_g[:, :], ALU.mult).then_inc(s_h, 1)

            def hT_lo(n):
                dve.wait_ge(s_hth, n + 1)
                v.tensor_tensor(hT[:, LO, :], PHT[:, 0:HC * P], hT[:, HI, :], ALU.subtract).then_inc(s_htl, 1)

            def blk(n, last=False):
                gated(n)
                if not last:
                    xT_lo(n + 1)
                hT_lo(n)

            def beside(n):
                routing_at(n)
                for u in halves_at(n):
                    convert(u // 2, u % 2, s_cvh, u)

            for q in range(NQ):
                x_stats(0, q)
            x_moments(0)
            parameters()
            step(None, 0, 1)
            for k in range(2):
                convert(SHARED, k, s_shh, k)
            with dve.Fori(0, B - 2) as b:
                step(b, b + 1, b + 2)
            step(B - 2, B - 1, None)
            step(B - 1, None, None)
            biased_logits()
            hT_lo(1)
            beside(1)
            for n in range(2, PEELED):
                blk(n)
                beside(n)
            with dve.Fori(PEELED // 2, NT // 2 - 1) as r:
                for k in range(2):
                    blk(2 * r + 1 + k)
                    convert(r + 1, k, s_cvh, 2 * r + 2 + k)
            with dve.Fori(NT // 2 - 1, (NB - 3) // 2) as r:
                for k in range(2):
                    blk(2 * r + 1 + k)
            blk(NB - 2)
            blk(NB - 1, last=True)

        @block.tensor
        def _(pe):
            t = nc.tensor

            def transposes(bank, src, count, s):
                for c in range(count):
                    last = t.transpose(bank[:, c * P:(c + 1) * P], src(c), ident[:, :])
                last.then_inc(s, 1)

            pe.wait_ge(s_const, CONSTS)
            pe.wait_ge(s_wqk, 16 * 2)
            transposes(RB, lambda c: wqk[:, c // CC, c % CC * P:(c % CC + 1) * P], 2 * CC, s_wT)
            pe.wait_ge(s_wTc, 1)

            def turn_context(b):
                pe.wait_ge(s_ctx, 16 * (b + 1))
                for c in range(CC):
                    need(pe, s_ef, 8 * b + c - 1)
                    transposes(EB[c], lambda n: ctx_sb[:, n, c * P:(c + 1) * P], NQ, s_eb)

            def project(b, m):
                pe.wait_ge(s_ef, 8 * b + CC)
                for c in range(CC):
                    last = t.matmul(EB[m][:, :], wqkT[:, m, c, :], ctxT[:, c, :], start=(c == 0), stop=(c == CC - 1))
                last.then_inc(s_eb, 1)

            def energy(b, q):
                pe.wait_ge(s_ef, 8 * b + max(4, 3 + q))
                t.matmul(EB[q % 2][:, :], qT[:, q * P:(q + 1) * P], kT, start=True, stop=True).then_inc(s_eb, 1)

            def turn_xn(b, q):
                pe.wait_ge(s_xn, NQ * b + q + 1)
                need(pe, s_xnl, NQ * b + q)
                transposes(TPX, lambda c: xn[:, q % 2, c * P:(c + 1) * P], DC, s_xnt)

            def turn_probs(b, q):
                pe.wait_ge(s_pn, NQ * b + q + 1)
                need(pe, s_pl, NQ * b + q)
                transposes(TPP, lambda c: prob[:, q % 2, c * P:(c + 1) * P], DC, s_pt)

            def turn_x2(b, q):
                pe.wait_ge(s_x2n, NQ * b + q + 1)
                one_before(pe, s_x2l, b, q)
                transposes(TPY, lambda c: x2n[:, q % 2, c * P:(c + 1) * P], DC, s_xt2)

            def attend(b, q):
                if q == 0:
                    pe.wait_ge(s_xnl, NQ * (b + 1))
                    pe.wait_ge(s_pl, NQ * (b + 1))
                two_before(pe, s_x2, b, q)
                bank = XM[q % 2]
                for c in range(DC):
                    chunk = xnt(b, HI, q, c)
                    t.matmul(bank[:, :], chunk, att(b, HI, c), start=(c == 0), stop=False)
                    t.matmul(bank[:, :], chunk, att(b, LO, c), start=False, stop=False)
                    last = t.matmul(bank[:, :], xnt(b, LO, q, c), att(b, HI, c), start=False, stop=(c == DC - 1))
                last.then_inc(s_xm, 1)

            def route_logits(b, q):
                pe.wait_ge(s_x2l, NQ * b + q + 1)
                dst = LG[:, q * E:(q + 1) * E]
                for c in range(DC):
                    hi, lo = (xT2[:, q % 2, l, c * P:(c + 1) * P] for l in (HI, LO))
                    t.matmul(dst, hi, wr16[:, HI, c, :], start=(c == 0), stop=False)
                    t.matmul(dst, hi, wr16[:, LO, c, :], start=False, stop=False)
                    last = t.matmul(dst, lo, wr16[:, HI, c, :], start=False, stop=(c == DC - 1))
                last.then_inc(s_lg, 1)

            def step(s2, s1, nx):
                for q in range(NQ):
                    if s1 is not None:
                        energy(s1, q)
                        turn_xn(s1, q)
                        if q > 0:
                            turn_probs(s1, q - 1)
                    elif q == 1:
                        turn_h(0)
                    if s2 is not None:
                        attend(s2, q)
                        if q > 1:
                            turn_x2(s2, q - 2)
                        if q > 2:
                            route_logits(s2, q - 3)
                if nx is not None:
                    turn_context(nx)
                elif s1 is not None:
                    turn_x(0, 0, 1)
                if s2 is not None:
                    turn_x2(s2, NQ - 2)
                if s1 is not None:
                    turn_probs(s1, NQ - 1)
                n = 0 if s1 is not None else 1
                if nx is not None:
                    project(nx, 0)
                else:
                    gate_up(n, shared)
                if s2 is not None:
                    turn_x2(s2, NQ - 1)
                    route_logits(s2, NQ - 3)
                if nx is not None:
                    project(nx, 1)
                else:
                    turn_x(n + 1, 1 - n, 1 + n)
                if s2 is not None:
                    route_logits(s2, NQ - 2)
                    route_logits(s2, NQ - 1)

            def positions():
                pe.wait_ge(s_sel, 1)
                t.matmul(RB[:, 0:TE], tri16[:, :], sel16, start=True, stop=False, skip_group_check=True)
                for j in range(NT):
                    rest = NT - j
                    last = t.matmul(RB[:, (j + 1) * E:(NT + 1) * E].rearrange("p (r e) -> p r e", e=E), ones16[:, :],
                                    sel16[:, j * E:(j + 1) * E].unsqueeze(1).broadcast_to([P, rest, E]),
                                    start=False, stop=(j == NT - 1), skip_group_check=True)
                last.then_inc(s_pos, 1)

            def table_rows():
                pe.wait_ge(s_1h, 1)
                table = RB[:, 0:4 * NR]
                for i in range(KT_N):
                    last = t.matmul(table, lane1h[:, i, :], blk1h[:, i, :, :].rearrange("p f n -> p (f n)"),
                                    start=(i == 0), stop=(i == KT_N - 1))
                last.then_inc(s_tab, 1)

            def gate_up(n, off):
                pe.wait_ge(s_xtl, n + 1)
                for c in range(DC):
                    hi, lo = (xT[:, l, c * P:(c + 1) * P] for l in (HI, LO))
                    for m, bank in enumerate((PG, PU)):
                        t.matmul(bank[:, 0:H], hi, gu_w(off, HI, m, c), start=(c == 0), stop=False)
                        t.matmul(bank[:, 0:H], hi, gu_w(off, LO, m, c), start=False, stop=False)
                    for m, bank in enumerate((PG, PU)):
                        last = t.matmul(bank[:, 0:H], lo, gu_w(off, HI, m, c), start=False, stop=(c == DC - 1))
                last.then_inc(s_gu, 1)

            def down(n, off):
                pe.wait_ge(s_htl, n + 1)
                need(pe, s_y, n)
                for j in range(HC):
                    hi, lo = (hT[0:HK[j], l, j * P:(j + 1) * P] for l in (HI, LO))
                    t.matmul(PY[:, :], hi, dn_w(off, HI, j), start=(j == 0), stop=False)
                    t.matmul(PY[:, :], hi, dn_w(off, LO, j), start=False, stop=False)
                    last = t.matmul(PY[:, :], lo, dn_w(off, HI, j), start=False, stop=(j == HC - 1))
                last.then_inc(s_dn, 1)

            def turn_x(n, i, gathered):
                if isinstance(n, int) and n == 0:
                    pe.wait_ge(s_xnl, NT)
                pe.wait_ge(s_xg[i], 16 * gathered)
                transposes(PXT, lambda c: xg[:, i, c * P:(c + 1) * P], DC, s_xt)

            def blk(n, i, gathered, off, before, beside=None):
                gate_up(n, off)
                if beside is not None:
                    beside()
                if gathered is not None:
                    turn_x(n + 1, 1 - i, gathered)
                down(n - 1, before)
                turn_h(n)

            def turn_h(n):
                pe.wait_ge(s_h, n + 1)
                transposes(PHT, lambda c: h[:, c * P:(c + 1) * P], HC, s_ht)

            def expert(n):
                return pe.value_load(eoff[0:1, bass.ds(n, 1)], min_val=0, max_val=E * SLOT)

            shared = SHARED * SLOT
            turn_context(0)
            project(0, 0)
            project(0, 1)
            step(None, 0, 1)
            pe.wait_ge(s_wrl, 1)
            with pe.Fori(0, B - 2) as b:
                step(b, b + 1, b + 2)
            pe.wait_ge(s_cvl, 2)
            step(B - 2, B - 1, None)
            step(B - 1, None, None)
            down(0, shared)
            turn_h(1)
            for n in range(2, PEELED):
                blk(n, n % 2, (n + 1) // 2 + 1, shared, shared, positions if n == POS_BLOCK else table_rows if n == TAB_BLOCK else None)
            with pe.Fori(PEELED // 2, NT // 2 - 1) as r:
                for k in range(2):
                    blk(2 * r + 1 + k, 1 - k, r + 2, shared, shared)
            blk(NT - 1, 1, NT // 2 + 1, shared, shared)
            pe.wait_ge(s_route, 1)
            pe.wait_ge(s_cvl, 2 + 2 * E)
            with pe.Fori(NT // 4, NB // 4) as r:
                for k in range(4):
                    n = 4 * r + k
                    blk(n, k % 2, 2 * r + (k + 1) // 2 + 1, expert(n), expert(n - 1))
            for n in range(NB // 4 * 4, NB):
                blk(n, n % 2, (n + 1) // 2 + 1 if n < NB - 1 else None, expert(n), expert(n - 1))
            down(NB - 1, expert(NB - 1))


_INS = ["x", "ctx_1024", "g_xattn", "g_ffn", "L0_xattn_Wq", "L0_xattn_bq", "L0_xattn_Wk", "L0_xattn_bk",
        "L0_ffn_Wg_s", "L0_ffn_Wu_s", "L0_ffn_Wd_s", "L0_ffn_Wg", "L0_ffn_Wu", "L0_ffn_Wd",
        "L0_ffn_Wr", "L0_ffn_br", "L0_ffn_rb"]


def kernel(**inputs):
    import numpy as np
    import concourse.bacc as bacc
    from concourse.bass_utils import run_bass_kernel_spmd

    nc = bacc.Bacc("TRN2", target_bir_lowering=False, num_devices=1)
    arrays, args = {}, []
    for name in _INS:
        a = np.ascontiguousarray(inputs[name])
        arrays[f"in_{name}"] = a
        args.append(nc.dram_tensor(f"in_{name}", a.shape, mybir.dt.from_np(a.dtype), kind="ExternalInput").ap())
    b, s, d = inputs["x"].shape
    out = nc.dram_tensor("out_rows", (b * s + P, d), F32, kind="ExternalOutput").ap()
    flamingo_block(nc, *args, out)
    got = run_bass_kernel_spmd(nc, [arrays], core_ids=[0]).results[0]["out_rows"]
    return got[:b * s].reshape(b, s, d)
```

```python
from contextlib import ExitStack

import concourse.bass as bass
from concourse import mybir

F32 = mybir.dt.float32
F16 = mybir.dt.float16
U32 = mybir.dt.uint32
I32 = mybir.dt.int32
ALU = mybir.AluOpType
ACT = mybir.ActivationFunctionType
AX_X = mybir.AxisListType.X

P = 128
EPS = 1e-5
WSCALE = 64.0
YSCALE = 1.0 / (WSCALE * WSCALE)
HI, LO = 0, 1


def flamingo_block(nc, x, ctx_in, g_x, g_f, wq, bq, wk, bk, wg_s, wu_s, wd_s, wg, wu, wd, wr, br, rb, out):
    B, S, D = x.shape
    C = ctx_in.shape[2]
    E, _, H = wg.shape
    T = B * S
    NQ = S // P
    NT = T // P
    DC = D // P
    CC = C // P
    HC = -(-H // P)
    HK = [min(P, H - P * j) for j in range(HC)]
    TOPK = 2
    NR = (TOPK * T + E * (P - 1)) // P
    NB = NT + NR
    assert (B, S, D, C, wq.shape[0], DC, NQ) == (4, 512, 512, 256, P, 4, 4) and NT % 2 == 0 and NR % 2 == 1

    GU_N = 2 * (DC // 2) * H
    DN_N = HC * (D // 2)
    HALF = GU_N + DN_N
    SLOT = 4 * HALF
    TAIL = NQ * 2 * D
    SHARED_AT = E * SLOT + TAIL

    x_v = x.rearrange("b (q p) d -> b p q d", p=P)
    ctx_v = ctx_in.rearrange("b (q p) c -> b p q c", p=P)
    x2n_rows = nc.dram_tensor("x2n_rows", [T, D], F32).ap()

    es = ExitStack()
    with es:
        def sb(name, shape, dt=F32):
            return es.enter_context(nc.sbuf_tensor(name, shape, dt))

        def sem(name):
            return es.enter_context(nc.semaphore(name))

        banks = [es.enter_context(nc.psum_tensor(f"bank{i}", [P, 512], F32)) for i in range(8)]
        EB, TP, XM, LG, RB = banks[0:2], banks[2:4], banks[4:6], banks[6], banks[7]
        TPX, TPP, TPY = TP[0], TP[1], RB
        TPY_LATE = XM[0]
        PG, PU, PXT, PHT, PY = EB[0], EB[1], TP[0], TP[1], XM[1]

        W = sb("W", [P, SHARED_AT + SLOT], F16)
        over32 = W[:, 0:SHARED_AT].bitcast(F32)
        at = [0]

        def carve(n):
            at[0] += n
            return at[0] - n

        def o32(n):
            o = carve(n)
            return over32[:, o:o + n]

        AT0 = 2 * carve(B * DC * S)
        XNT0 = 2 * carve(B * DC * S)
        ABS = 2 * DC * S
        x2 = o32(2 * D).rearrange("p (i n) -> p i n", i=2)
        x2n = o32(2 * D).rearrange("p (i n) -> p i n", i=2)
        POS_BLOCK, TAB_BLOCK = 4, 8
        PEELED = TAB_BLOCK + 1
        ROUTE0 = (TAB_BLOCK + 2) * HALF
        assert at[0] <= ROUTE0
        ctx_sb = o32(NQ * C).rearrange("p (q c) -> p q c", q=NQ)
        ctxT = o32(CC * S).rearrange("p (c n) -> p c n", c=CC)
        qT, kT = o32(S), o32(S)
        prob = o32(2 * S).rearrange("p (i n) -> p i n", i=2)
        xn = o32(2 * D).rearrange("p (i n) -> p i n", i=2)
        X0 = SHARED_AT // 2 - B * NQ * D
        assert at[0] <= X0
        x_sb = over32[:, X0:X0 + B * NQ * D]

        def xT2(n, l):
            return W[:, bass.ds(n * (2 * D) + (2 * X0 + l * D), D)]

        def xT2_chunk(n, l, c):
            return W[:, bass.ds(n * (2 * D) + (2 * X0 + l * D + c * P), P)]

        rt = [ROUTE0]

        def r32(n):
            rt[0] += n
            assert rt[0] <= X0
            return over32[:, rt[0] - n:rt[0]]

        def r16(n):
            return r32((n + 1) // 2).bitcast(F16)

        TE = NT * E
        KT_N = TOPK * NT
        logits = sb("logits", [P, TE])
        lrb, pr = r32(TE), r32(TE)
        eqv, pr2, best = r32(TE), r32(TE), r32(NT)
        selk, prodk = r32(TOPK * TE), r32(TOPK * TE)
        topv, wk_f = r32(KT_N), r32(KT_N)
        vsum, vinv = r32(NT), r32(NT)
        sel16 = r16(TE)
        whi, wlo = r16(KT_N), r16(KT_N)
        cgt, endm = r32(E * NT), r32(E * E)
        nblk, endb, startb = r32(E), r32(E), r32(E)
        slot_te, slotk = r32(TE), r32(KT_N)
        slot_i, lane_i, blk_i = (r32(KT_N).bitcast(I32) for _ in range(3))
        lane1h = r16(KT_N * P).rearrange("p (i l) -> p i l", l=P)
        blk1h = r16(KT_N * 4 * NR).rearrange("p (i f n) -> p i f n", f=4, n=NR)
        tgt_f, w_f = r32(NR), r32(NR)
        eb_m, eb_f = r32(NR * E), r32(NR)

        tok = sb("tok", [P, NR], U32)
        tgt = sb("tgt", [P, NB], U32)
        wcol = sb("wcol", [P, NB])
        eoff = sb("eoff", [1, NB], I32)

        stage = sb("stage", [P, 2, HALF])
        xg = sb("xg", [P, 2, D])
        xT = sb("xT", [P, 2, D], F16)
        silu_g = sb("silu_g", [P, H])
        h = sb("h", [P, HC * P])
        hT = sb("hT", [P, 2, HC * P], F16)
        y = sb("y", [P, 2, D])
        idx_g = sb("idx_g", [P, 2], U32)
        idx_s = sb("idx_s", [P, 2], U32)

        ident = sb("ident", [P, P])
        ones16 = sb("ones16", [P, P], F16)
        tri16 = sb("tri16", [P, P], F16)
        lane_iota = sb("lane_iota", [P, P])
        cnt_iota = sb("cnt_iota", [P, NT])
        rev_e = sb("rev_e", [P, E])
        tri_le = sb("tri_le", [P, E, E])
        tok_id = sb("tok_id", [P, KT_N])
        pad_row = sb("pad_row", [P, 1])
        pad_neg = sb("pad_neg", [P, 1])
        mhalf = sb("mhalf", [P, NQ])
        wqk = sb("wqk", [P, 2, C])
        wqkT = sb("wqkT", [P, 2, CC, P])
        bqk = sb("bqk", [P, 2])
        gates = sb("gates", [P, 2])
        tanh_g = sb("tanh_g", [P, 2])
        gff = sb("gff", [P, 1])
        br_sb, rb_sb = sb("br_sb", [P, E]), sb("rb_sb", [P, E])
        wr_sb = sb("wr_sb", [P, DC, E])
        wr16 = sb("wr16", [P, 2, DC, E], F16)

        st1, mv1 = sb("st1", [P, NQ, 6]), sb("mv1", [P, NQ, 2])
        ve1, nm1, rstd1, nb1 = (sb(n, [P, NQ]) for n in ("ve1", "nm1", "rstd1", "nb1"))
        st2, mv2 = sb("st2", [P, 2, 6]), sb("mv2", [P, 2, 2])
        ve2, nm2, rstd2, nb2 = (sb(n, [P, 2]) for n in ("ve2", "nm2", "rstd2", "nb2"))
        negmax, rowsum, rinv = (sb(n, [P, NQ]) for n in ("negmax", "rowsum", "rinv"))

        s_const = sem("s_const")
        s_wqk = sem("s_wqk")
        s_par = sem("s_par")
        s_x = sem("s_x")
        s_ctx = sem("s_ctx")
        s_wT, s_wTc = sem("s_wT"), sem("s_wTc")
        s_tanh, s_gff = sem("s_tanh"), sem("s_gff")
        s_wrh, s_wrl = sem("s_wrh"), sem("s_wrl")
        s_eb, s_ef = sem("s_eb"), sem("s_ef")
        s_xnt, s_pt, s_xt2 = sem("s_xnt"), sem("s_pt"), sem("s_xt2")
        s_xnh, s_xnl = sem("s_xnh"), sem("s_xnl")
        s_ph, s_pl = sem("s_ph"), sem("s_pl")
        s_x2h, s_x2l = sem("s_x2h"), sem("s_x2l")
        s_max, s_rec, s_pn = sem("s_max"), sem("s_rec"), sem("s_pn")
        s_bn1, s_ag1, s_v1 = sem("s_bn1"), sem("s_ag1"), sem("s_v1")
        s_bn2, s_ag2, s_v2 = sem("s_bn2"), sem("s_ag2"), sem("s_v2")
        s_pow1, s_n1 = sem("s_pow1"), sem("s_n1")
        s_pow2, s_n2 = sem("s_pow2"), sem("s_n2")
        s_xn, s_x2n = sem("s_xn"), sem("s_x2n")
        s_xm, s_x2 = sem("s_xm"), sem("s_x2")
        s_lg, s_lgf = sem("s_lg"), sem("s_lgf")
        s_st_x2 = [sem("s_st_x2_0"), sem("s_st_x2_1")]
        s_st_n = [sem("s_st_n_0"), sem("s_st_n_1")]
        s_pad = sem("s_pad")
        s_ch = sem("s_ch")
        s_lrb, s_ex = sem("s_lrb"), sem("s_ex")
        s_sel, s_pos, s_1h, s_tab = sem("s_sel"), sem("s_pos"), sem("s_1h"), sem("s_tab")
        s_b1h, s_bf = sem("s_b1h"), sem("s_bf")
        s_route = sem("s_route")
        s_stg = [sem("s_stg_0"), sem("s_stg_1")]
        s_shh = [sem("s_shh_0"), sem("s_shh_1")]
        s_cvh, s_cvl = sem("s_cvh"), sem("s_cvl")
        s_zero = sem("s_zero")
        s_idxg, s_idxs = sem("s_idxg"), sem("s_idxs")
        s_xg = [sem("s_xg_0"), sem("s_xg_1")]
        s_xt, s_xth, s_xtl = sem("s_xt"), sem("s_xth"), sem("s_xtl")
        s_gu, s_silu, s_h = sem("s_gu"), sem("s_silu"), sem("s_h")
        s_ht, s_hth, s_htl = sem("s_ht"), sem("s_hth"), sem("s_htl")
        s_apart = sem("s_apart")
        s_dn, s_y = sem("s_dn"), sem("s_y")
        s_sc = sem("s_sc")

        assert SLOT <= (B - 1) * ABS and 2 * E == NT
        assert all(2 * X0 + n * 2 * D >= (n + 1) * 2 * HALF for n in range(NT))

        block = es.enter_context(nc.Block())

        def need(eng, s, v):
            if not isinstance(v, int) or v > 0:
                eng.wait_ge(s, v)

        CONSTS, PARS = 14, 7

        def wait_apart(eng, s, v):
            eng.wait_ge(s, v)
            eng.sem_inc(s_apart, 1)

        def x2_bank(q):
            return TPY_LATE if q == NQ - 2 else TPY

        def two_before(eng, s, b, q):
            if q > 1:
                eng.wait_ge(s, NQ * b + q - 1)

        def stored_before(eng, s, b, q):
            if q > 1 or isinstance(b, int) and b > 0:
                eng.wait_ge(s[q % 2], 16 * (NQ // 2 * b + q // 2))

        def all_stored(eng, s, b):
            for i in range(2):
                eng.wait_ge(s[i], 16 * (NQ // 2) * (b + 1))

        def rows(b, q):
            return bass.ds(b * (NQ * D) + q * D, D)

        def xnt(b, hl, q, c=None):
            o = XNT0 + b * ABS + (hl * DC * S + q * D)
            return W[:, bass.ds(o, D)] if c is None else W[:, bass.ds(o + c * P, P)]

        def att(b, hl, c):
            return W[:, bass.ds(AT0 + b * ABS + (hl * DC * S + c * S), S)]

        def att_cols(b, hl, q):
            whole = W[:, bass.ds(AT0 + b * ABS + hl * DC * S, DC * S)]
            return whole.rearrange("p (c m) -> p c m", c=DC)[:, :, q * P:(q + 1) * P]

        def gu_w(off, hl, m, c):
            k, c2 = divmod(c, DC // 2)
            return W[:, bass.ds(off + (k * 2 * HALF + hl * HALF + (m * (DC // 2) + c2) * H), H)]

        def dn_w(off, hl, j):
            whole = W[:, bass.ds(off, SLOT)].rearrange("p (k r) -> p k r", k=2)
            o = hl * HALF + GU_N + j * (D // 2)
            return whole[0:HK[j], :, o:o + D // 2]

        wg_rows, wu_rows, wd_rows = (w.rearrange("e d n -> (e d) n") for w in (wg, wu, wd))

        @block.sync
        def _(sp):
            def stage_half(k, gate, up, down):
                half = stage[:, k, 0:GU_N].rearrange("p (m c n) -> p m c n", m=2, c=DC // 2)
                rest = stage[:, k, GU_N:HALF].rearrange("p (j n) -> p j n", j=HC)
                sp.dma_start(half[:, 0], gate.rearrange("(c p) n -> p c n", p=P)).then_inc(s_stg[k], 16)
                sp.dma_start(half[:, 1], up.rearrange("(c p) n -> p c n", p=P)).then_inc(s_stg[k], 16)
                sp.dma_start(rest[:, 0:HC - 1], down[0].rearrange("(j p) n -> p j n", p=P)).then_inc(s_stg[k], 16)
                sp.dma_start(rest[0:HK[-1], HC - 1], down[1]).then_inc(s_stg[k], 16)

            def load_ctx(b):
                need(sp, s_eb, 8 * (b - 1) + CC)
                sp.dma_start(ctx_sb, ctx_v[b]).then_inc(s_ctx, 16)

            def load_x(b):
                need(sp, s_x, 16 * b)
                sp.dma_start(x_sb[:, b * NQ * D:(b + 1) * NQ * D].rearrange("p (q d) -> p q d", q=NQ),
                             x_v[b]).then_inc(s_x, 16)

            def store_x2(b, q):
                sp.wait_ge(s_x2, NQ * b + q + 1)
                sp.dma_start(out[bass.ds(b * S + q * P, P), :], x2[:, q % 2, :]).then_inc(s_st_x2[q % 2], 16)

            def store_x2n(b, q):
                sp.wait_ge(s_x2n, NQ * b + q + 1)
                sp.dma_start(x2n_rows[bass.ds(b * S + q * P, P), :], x2n[:, q % 2, :]).then_inc(s_st_n[q % 2], 16)

            def store(b, tiles=range(NQ)):
                for q in tiles:
                    store_x2(b, q)
                    store_x2n(b, q)

            def stage_routed(e, k):
                sp.wait_ge(s_cvl, 2 if isinstance(e, int) and e == 0 else 2 * e + k + 1)
                cols = slice(k * (D // 2), (k + 1) * (D // 2))
                rows_k = bass.ds(e * D + k * (D // 2), D // 2)
                stage_half(k, wg_rows[rows_k, :], wu_rows[rows_k, :],
                           (wd_rows[bass.ds(e * H, (HC - 1) * P), cols],
                            wd_rows[bass.ds(e * H + (HC - 1) * P, HK[-1]), cols]))

            load_ctx(0)
            for m, src in enumerate((wq, wk)):
                sp.dma_start(wqk[:, m, :], src).then_inc(s_wqk, 16)
            load_x(0)
            for dst, src in ((bqk[:, 0:1], bq.rearrange("(p a) -> p a", a=1)), (bqk[:, 1:2], bk.rearrange("(p a) -> p a", a=1)),
                             (gates[:, 0:1], g_x.partition_broadcast(P)), (gates[:, 1:2], g_f.partition_broadcast(P)),
                             (br_sb[:, :], br.partition_broadcast(P)), (rb_sb[:, :], rb.partition_broadcast(P)),
                             (wr_sb[:, :, :], wr.rearrange("(c p) e -> p c e", p=P))):
                sp.dma_start(dst, src).then_inc(s_par, 16)
            sp.wait_ge(s_zero, 3)
            for k in (1, 0):
                rows_k = slice(k * (D // 2), (k + 1) * (D // 2))
                stage_half(k, wg_s[rows_k, :], wu_s[rows_k, :],
                           (wd_s[0:(HC - 1) * P, rows_k], wd_s[(HC - 1) * P:H, rows_k]))
                if k == 1:
                    load_x(1)
            load_ctx(1)
            load_x(2)
            load_x(3)
            sp.dma_start(out[T:T + P, :], y[:, 0, :]).then_inc(s_pad, 16)
            load_ctx(2)
            for k in range(2):
                stage_routed(0, k)
            store(0)
            load_ctx(3)
            with sp.Fori(1, B - 1) as b:
                store(b)
            store(B - 1, range(1))
            store_x2(B - 1, 1)
            stage_routed(1, 0)
            store_x2n(B - 1, 1)
            store(B - 1, range(2, NQ))
            stage_routed(1, 1)
            with sp.Fori(2, E) as e:
                for k in range(2):
                    stage_routed(e, k)
            sp.wait_ge(s_pad, 16)
            sp.wait_ge(s_sc, 16 * NB)

        @block.gpsimd
        def _(pool):
            g = nc.gpsimd
            iota = dict(allow_small_or_imprecise_dtypes=True)
            g.memset(ident[:, :], 0.0).then_inc(s_const, 1)
            g.memset(ones16[:, :], 1.0).then_inc(s_const, 1)
            g.memset(mhalf[:, :], -0.5).then_inc(s_const, 1)
            g.memset(tri_le[:, :, :], 1.0).then_inc(s_const, 1)
            g.iota(lane_iota[:, :], [[1, P]], base=0, channel_multiplier=0, **iota).then_inc(s_const, 1)
            g.iota(cnt_iota[:, :], [[P, NT]], base=0, channel_multiplier=0, **iota).then_inc(s_const, 1)
            g.iota(tok_id[:, :], [[0, TOPK], [P, NT]], base=0, channel_multiplier=1, **iota).then_inc(s_const, 1)
            g.iota(rev_e[:, :], [[-1, E]], base=E, channel_multiplier=0, **iota).then_inc(s_const, 1)
            g.iota(pad_row[:, :], [[0, 1]], base=T, channel_multiplier=1, **iota).then_inc(s_const, 1)
            g.iota(pad_neg[:, :], [[0, 1]], base=-T, channel_multiplier=-1, **iota).then_inc(s_const, 1)
            g.iota(tgt[:, 0:NT], [[P, NT]], base=0, channel_multiplier=1).then_inc(s_const, 1)
            pool.wait_ge(s_const, 11)
            g.affine_select(out=ident[:, :], in_=ident[:, :], compare_op=ALU.not_equal, fill=1.0,
                            base=0, pattern=[[-1, P]], channel_multiplier=1).then_inc(s_const, 1)
            g.affine_select(out=tri16[:, :], in_=ones16[:, :], compare_op=ALU.is_gt, fill=0.0,
                            base=0, pattern=[[1, P]], channel_multiplier=-1).then_inc(s_const, 1)
            g.affine_select(out=tri_le[:, :, :], in_=tri_le[:, :, :], compare_op=ALU.is_ge, fill=0.0,
                            base=0, pattern=[[1, E], [-1, E]], channel_multiplier=0).then_inc(s_const, 1)
            pool.wait_ge(s_const, CONSTS)

            def scale_x(b):
                pool.wait_ge(s_v1, b + 1)
                need(pool, s_xn, NQ * b)
                g.tensor_tensor(rstd1[:, :], ve1[:, :], mhalf[:, :], ALU.pow).then_inc(s_pow1, 1)
                pool.wait_ge(s_pow1, b + 1)
                g.tensor_tensor(nb1[:, :], nm1[:, :], rstd1[:, :], ALU.mult).then_inc(s_n1, 1)

            def scale_x2(b, q):
                i = slice(q % 2, q % 2 + 1)
                pool.wait_ge(s_v2, NQ * b + q + 1)
                two_before(pool, s_x2n, b, q)
                g.tensor_tensor(rstd2[:, i], ve2[:, i], mhalf[:, 0:1], ALU.pow).then_inc(s_pow2, 1)
                pool.wait_ge(s_pow2, NQ * b + q + 1)
                g.tensor_tensor(nb2[:, i], nm2[:, i], rstd2[:, i], ALU.mult).then_inc(s_n2, 1)

            def step(s2, nx):
                if s2 is not None:
                    for q in range(NQ):
                        scale_x2(s2, q)
                if nx is not None:
                    scale_x(nx)

            def gather(n, i):
                need(pool, s_xt, n - NT - 1)
                g.tensor_copy(idx_g[:, i:i + 1], tok[:, bass.ds(n - NT, 1)]).then_inc(s_idxg, 1)
                wait_apart(pool, s_idxg, n - NT + 1)
                g.indirect_dma_start(xg[:, i, :], None, x2n_rows,
                                     bass.IndirectOffsetOnAxis(ap=idx_g[:, i:i + 1], axis=0)).then_inc(s_xg[i], 16)

            def scatter(n, i):
                g.tensor_copy(idx_s[:, i:i + 1], tgt[:, bass.ds(n, 1)]).then_inc(s_idxs, 1)
                pool.wait_ge(s_idxs, n + 1)
                need(pool, s_sc, 16 * n)
                wait_apart(pool, s_y, n + 1)
                g.indirect_dma_start(out, bass.IndirectOffsetOnAxis(ap=idx_s[:, i:i + 1], axis=0), y[:, i, :],
                                     None, compute_op=ALU.add).then_inc(s_sc, 16)

            scale_x(0)
            pool.wait_ge(s_n1, 1)
            for q in range(NQ):
                need(pool, s_xnt, q - 1)
                g.tensor_scalar(xn[:, q % 2, :], x_sb[:, q * D:(q + 1) * D], rstd1[:, q:q + 1], nb1[:, q:q + 1],
                                ALU.mult, ALU.add).then_inc(s_xn, 1)
            pool.wait_ge(s_stg[0], 64)
            g.tensor_scalar(W[:, SHARED_AT:SHARED_AT + HALF], stage[:, 0, :], WSCALE, None, ALU.mult).then_inc(s_shh[0], 1)
            step(None, 1)
            with pool.Fori(0, B - 2) as b:
                step(b, b + 2)
            step(B - 2, None)
            step(B - 1, None)
            all_stored(pool, s_st_x2, B - 1)
            pool.wait_ge(s_pad, 16)
            LEAD = 4
            for n in range(2):
                scatter(n, n % 2)
            with pool.Fori(1, POS_BLOCK // 2) as r:
                for i in range(2):
                    scatter(2 * r + i, i)
            pool.wait_ge(s_b1h, 1)
            for f, z in enumerate((tok_id[:, :], whi, wlo)):
                g.tensor_tensor(blk1h[:, :, f + 1, :], blk1h[:, :, 0, :], z.unsqueeze(2).broadcast_to([P, KT_N, NR]),
                                ALU.mult).then_inc(s_bf, 1)
            with pool.Fori(POS_BLOCK // 2, (NT - LEAD) // 2) as r:
                for i in range(2):
                    scatter(2 * r + i, i)
            all_stored(pool, s_st_n, B - 1)
            pool.wait_ge(s_route, 1)
            for n in range(NT - LEAD, NT - LEAD + 2):
                scatter(n, n % 2)
                gather(n + LEAD, n % 2)
            with pool.Fori((NT - LEAD) // 2 + 1, (NB - LEAD - 1) // 2) as r:
                for i in range(2):
                    scatter(2 * r + i, i)
                    gather(2 * r + i + LEAD, i)
            for n in range(NB - LEAD - 1, NB):
                scatter(n, n % 2)
                if n + LEAD < NB:
                    gather(n + LEAD, n % 2)

        @block.scalar
        def _(act):
            a = nc.scalar
            def context(b, c):
                act.wait_ge(s_eb, 8 * b + c + 1)
                a.activation(ctxT[:, c, :], EB[c][:, :], ACT.Copy).then_inc(s_ef, 1)

            def project(b, m):
                act.wait_ge(s_eb, 8 * b + CC + m + 1)
                a.activation((qT, kT)[m], EB[m][:, :], ACT.Identity, bias=bqk[:, m:m + 1]).then_inc(s_ef, 1)

            def normalise(b, q):
                if q == 0:
                    act.wait_ge(s_n1, b + 1)
                need(act, s_xnt, NQ * b + q - 1)
                a.activation(xn[:, q % 2, :], x_sb[:, rows(b, q)], ACT.Identity, bias=nb1[:, q:q + 1],
                             scale=rstd1[:, q:q + 1]).then_inc(s_xn, 1)

            def xn_hi(b, q):
                act.wait_ge(s_xnt, NQ * b + q + 1)
                a.activation(xnt(b, HI, q), TPX[:, :], ACT.Copy).then_inc(s_xnh, 1)

            def exponentials(b, q):
                act.wait_ge(s_max, NQ * b + q + 1)
                need(act, s_pt, NQ * b + q - 1)
                a.activation(prob[:, q % 2, :], EB[q % 2][:, :], ACT.Exp, bias=negmax[:, q:q + 1],
                             accum_out=rowsum[:, q:q + 1]).then_inc(s_ef, 1)

            def scale_probs(b, q):
                act.wait_ge(s_rec, NQ * b + q + 1)
                a.activation(prob[:, q % 2, :], prob[:, q % 2, :], ACT.Copy, scale=rinv[:, q:q + 1]).then_inc(s_pn, 1)

            def probs_hi(b, q):
                act.wait_ge(s_pt, NQ * b + q + 1)
                a.activation(att_cols(b, HI, q), TPP[:, :].rearrange("p (c m) -> p c m", c=DC), ACT.Copy).then_inc(s_ph, 1)

            def normalise_x2(b, q):
                i = q % 2
                act.wait_ge(s_n2, NQ * b + q + 1)
                two_before(act, s_xt2, b, q)
                stored_before(act, s_st_n, b, q)
                a.activation(x2n[:, i, :], x2[:, i, :], ACT.Identity, bias=nb2[:, i:i + 1],
                             scale=rstd2[:, i:i + 1]).then_inc(s_x2n, 1)

            def x2_hi(b, q):
                act.wait_ge(s_xt2, NQ * b + q + 1)
                a.activation(xT2(NQ * b + q, HI), x2_bank(q)[:, :], ACT.Copy).then_inc(s_x2h, 1)

            def step(s2, s1, nx):
                for q in range(NQ):
                    if s1 is not None:
                        xn_hi(s1, q)
                        exponentials(s1, q)
                        if s2 is not None and q < NQ - 1:
                            normalise(s1, q + 1)
                        if q > 0:
                            probs_hi(s1, q - 1)
                        scale_probs(s1, q)
                    elif q == 1:
                        hT_hi(0)
                        routed_half(1)
                    if s2 is not None and nx is not None and q == NQ - 1:
                        break
                    if s2 is not None and q > 0:
                        normalise_x2(s2, q - 1)
                    if s2 is not None and q > 1:
                        x2_hi(s2, q - 2)
                    if s1 is None and q == 0:
                        routed_half(0)
                if nx is not None:
                    for c in range(CC):
                        context(nx, c)
                    if s2 is not None:
                        x2_hi(s2, NQ - 3)
                        normalise_x2(s2, NQ - 2)
                    probs_hi(s1, NQ - 1)
                    if s2 is not None:
                        x2_hi(s2, NQ - 2)
                        normalise_x2(s2, NQ - 1)
                    project(nx, 0)
                    if s2 is not None:
                        x2_hi(s2, NQ - 1)
                    normalise(nx, 0)
                    project(nx, 1)
                else:
                    x2_hi(s2, NQ - 2)
                    if s1 is not None:
                        probs_hi(s1, NQ - 1)
                    normalise_x2(s2, NQ - 1)
                    if s1 is None:
                        routed_half(2)
                    x2_hi(s2, NQ - 1)
                    silu(0 if s1 is not None else 1)
                if s2 is not None and nx is not None:
                    all_stored(act, s_st_n, s2)

            def convert(slot, k, loads):
                act.wait_ge(s_stg[k], 64 * loads)
                dst = W[:, bass.ds(slot * SLOT + k * 2 * HALF, HALF)]
                a.activation(dst, stage[:, k, :], ACT.Copy, scale=WSCALE).then_inc(s_cvh, 1)

            def xT_hi(n):
                act.wait_ge(s_xt, n - NT + 1)
                a.activation(xT[:, HI, :], PXT[:, :], ACT.Copy).then_inc(s_xth, 1)

            def y_out(n, i):
                act.wait_ge(s_dn, n + 1)
                need(act, s_sc, 16 * (n - 1))
                a.activation(y[:, i, :], PY[:, :], ACT.Copy, scale=wcol[:, bass.ds(n, 1)]).then_inc(s_y, 1)

            def silu(n):
                act.wait_ge(s_gu, n + 1)
                need(act, s_h, n)
                a.activation(silu_g[:, :], PG[:, 0:H], ACT.Silu, scale=1.0 / WSCALE).then_inc(s_silu, 1)

            def hT_hi(n):
                act.wait_ge(s_ht, n + 1)
                a.activation(hT[:, HI, :], PHT[:, 0:HC * P], ACT.Copy).then_inc(s_hth, 1)

            def blk(n, i, turn=False):
                silu(n)
                if turn:
                    xT_hi(n + 1)
                y_out(n - 1, 1 - i)
                hT_hi(n)

            def routed_half(u):
                if u == 0:
                    act.wait_ge(s_x2, NQ * (B - 1))
                if u == 2:
                    act.wait_ge(s_x2, NT)
                if u == 3:
                    all_stored(act, s_st_x2, B - 1)
                    all_stored(act, s_st_n, B - 1)
                convert(u // 2, u % 2, u // 2 + 2)

            for c in range(CC):
                context(0, c)
            act.wait_ge(s_wT, 1)
            a.activation(wqkT[:, :, :, :].rearrange("p a c d -> p (a c d)"), RB[:, 0:2 * C], ACT.Copy).then_inc(s_wTc, 1)
            act.wait_ge(s_par, 16 * PARS)
            project(0, 0)
            project(0, 1)
            a.activation(tanh_g[:, :], gates[:, :], ACT.Tanh).then_inc(s_tanh, 1)
            a.activation(wr16[:, HI], wr_sb[:, :, :], ACT.Copy, scale=WSCALE).then_inc(s_wrh, 1)
            act.wait_ge(s_stg[1], 64)
            o = SHARED_AT + 2 * HALF
            a.activation(W[:, o:o + HALF], stage[:, 1, :], ACT.Copy, scale=WSCALE).then_inc(s_shh[1], 1)
            step(None, 0, 1)
            with act.Fori(0, B - 2) as b:
                step(b, b + 1, b + 2)
            step(B - 2, B - 1, None)
            step(B - 1, None, None)

            act.wait_ge(s_pad, 16)
            y_out(0, 0)
            hT_hi(1)
            act.wait_ge(s_lrb, 1)
            a.activation(pr, lrb, ACT.Exp, scale=-1.0).then_inc(s_ex, 1)
            for n in range(2, PEELED):
                blk(n, n % 2)
                routed_half(n + 1)
            act.wait_ge(s_route, 1)
            with act.Fori(PEELED // 2, NT // 2 - 1) as r:
                for k in range(2):
                    blk(2 * r + 1 + k, 1 - k)
                    convert(r + 1, k, r + 3)
            blk(NT - 1, 1, turn=True)
            with act.Fori(NT // 2, (NB - 1) // 2) as r:
                for i in range(2):
                    blk(2 * r + i, i, turn=True)
            blk(NB - 1, 0)
            y_out(NB - 1, (NB - 1) % 2)

        @block.vector
        def _(dve):
            v = nc.vector
            chain = [0]

            def link(ins):
                chain[0] += 1
                ins.then_inc(s_ch, 1)
                dve.wait_ge(s_ch, chain[0])

            for k in range(2):
                v.memset(stage[96:P, k, GU_N:HALF], 0.0).then_inc(s_zero, 1)
            v.memset(y[:, 0, :], 0.0).then_inc(s_zero, 1)
            v.memset(h[:, :], 0.0)
            v.memset(eoff[0:1, 0:NT], SHARED_AT)

            def parameters():
                dve.wait_ge(s_tanh, 1)
                link(v.tensor_scalar(gff[:, :], tanh_g[:, 1:2], YSCALE, None, ALU.mult))
                v.tensor_copy(wcol[:, 0:NT], gff[:, :].broadcast_to([P, NT]))
                dve.wait_ge(s_wrh, 1)
                v.scalar_tensor_tensor(wr16[:, LO].rearrange("p c e -> p (c e)"), wr_sb[:, :, :].rearrange("p c e -> p (c e)"), WSCALE,
                                       wr16[:, HI].rearrange("p c e -> p (c e)"), ALU.mult, ALU.subtract).then_inc(s_wrl, 1)

            def logits_out(b):
                dve.wait_ge(s_lg, NQ * (b + 1))
                to = logits[:, bass.ds(b * NQ * E, NQ * E)].rearrange("p (q e) -> p q e", e=E)
                v.scalar_tensor_tensor(to, LG[:, 0:NQ * E].rearrange("p (q e) -> p q e", e=E), 1.0 / WSCALE,
                                       br_sb[:, :].unsqueeze(1).broadcast_to([P, NQ, E]), ALU.mult, ALU.add).then_inc(s_lgf, 1)

            def routed_half(u):
                convert(u // 2 * SLOT, u % 2, s_cvh, u)

            def x_stats(b, q):
                if q == 0:
                    dve.wait_ge(s_x, 16 * (b + 1))
                v.bn_stats(st1[:, q, :], x_sb[:, rows(b, q)]).then_inc(s_bn1, 1)

            def x_moments(b):
                need(dve, s_n1, b)
                wait_apart(dve, s_bn1, NQ * (b + 1))
                for q in range(NQ):
                    v.bn_aggr(mv1[:, q, :], st1[:, q, :]).then_inc(s_ag1, 1)
                dve.wait_ge(s_ag1, NQ * (b + 1))
                v.tensor_scalar(ve1[:, :], mv1[:, :, 1], EPS, None, ALU.add)
                v.tensor_scalar(nm1[:, :], mv1[:, :, 0], -1.0, None, ALU.mult).then_inc(s_v1, 1)

            def row_max(b, q):
                dve.wait_ge(s_eb, 8 * b + 5 + q)
                need(dve, s_ef, 8 * (b - 1) + 5 + q)
                v.reduce_max(negmax[:, q:q + 1], EB[q % 2][:, :], axis=AX_X, negate=True).then_inc(s_max, 1)

            def row_rec(b, q):
                dve.wait_ge(s_ef, 8 * b + 5 + q)
                need(dve, s_pn, NQ * (b - 1) + q + 1)
                v.reciprocal(rinv[:, q:q + 1], rowsum[:, q:q + 1]).then_inc(s_rec, 1)

            def xn_lo(b, q):
                dve.wait_ge(s_xnh, NQ * b + q + 1)
                v.tensor_tensor(xnt(b, LO, q), TPX[:, :], xnt(b, HI, q), ALU.subtract).then_inc(s_xnl, 1)

            def probs_lo(b, q):
                dve.wait_ge(s_ph, NQ * b + q + 1)
                v.tensor_tensor(att_cols(b, LO, q), TPP[:, :].rearrange("p (c m) -> p c m", c=DC), att_cols(b, HI, q),
                                ALU.subtract).then_inc(s_pl, 1)

            def x2_lo(b, q):
                dve.wait_ge(s_x2h, NQ * b + q + 1)
                v.tensor_tensor(xT2(NQ * b + q, LO), x2_bank(q)[:, :], xT2(NQ * b + q, HI), ALU.subtract).then_inc(s_x2l, 1)

            def add_attention(b, q):
                i = q % 2
                dve.wait_ge(s_xm, NQ * b + q + 1)
                two_before(dve, s_x2n, b, q)
                stored_before(dve, s_st_x2, b, q)
                v.scalar_tensor_tensor(x2[:, i, :], XM[i][:, :], tanh_g[:, 0:1], x_sb[:, rows(b, q)],
                                       ALU.mult, ALU.add).then_inc(s_x2, 1)
                dve.wait_ge(s_x2, NQ * b + q + 1)
                v.bn_stats(st2[:, i, :], x2[:, i, :]).then_inc(s_bn2, 1)

            def x2_moments(b, q):
                i = q % 2
                wait_apart(dve, s_bn2, NQ * b + q + 1)
                v.bn_aggr(mv2[:, i, :], st2[:, i, :]).then_inc(s_ag2, 1)
                two_before(dve, s_n2, b, q)
                dve.wait_ge(s_ag2, NQ * b + q + 1)
                v.tensor_scalar(ve2[:, i:i + 1], mv2[:, i, 1:2], EPS, None, ALU.add)
                v.tensor_scalar(nm2[:, i:i + 1], mv2[:, i, 0:1], -1.0, None, ALU.mult).then_inc(s_v2, 1)

            def step(s2, s1, nx):
                for q in range(NQ):
                    if s1 is not None:
                        row_max(s1, q)
                    if s2 is not None and q > 0:
                        x2_moments(s2, q - 1)
                    if s1 is None and q == 1:
                        hT_lo(0)
                    if s2 is not None and q > 2:
                        x2_lo(s2, q - 3)
                    if s1 is not None:
                        xn_lo(s1, q)
                        row_rec(s1, q)
                    if nx is not None:
                        x_stats(nx, q)
                    if s1 is not None and q > 0:
                        probs_lo(s1, q - 1)
                    if s2 is not None:
                        add_attention(s2, q)
                    if s1 is None and q == 0:
                        routed_half(0)
                if s2 is not None:
                    x2_lo(s2, NQ - 3)
                if nx is not None:
                    if s2 is not None:
                        x2_moments(s2, NQ - 1)
                    probs_lo(s1, NQ - 1)
                    if s2 is not None:
                        x2_lo(s2, NQ - 2)
                    x_moments(nx)
                    if s2 is not None:
                        x2_lo(s2, NQ - 1)
                else:
                    x2_moments(s2, NQ - 1)
                    x2_lo(s2, NQ - 2)
                    if s1 is not None:
                        probs_lo(s1, NQ - 1)
                    else:
                        routed_half(1)
                    x2_lo(s2, NQ - 1)
                    gated(0 if s1 is not None else 1)
                if s2 is not None:
                    logits_out(s2)
                    if nx is not None:
                        all_stored(dve, s_st_x2, s2)

            def convert(at_slot, k, s_high, u):
                dve.wait_ge(s_high, u + 1)
                o = at_slot + k * 2 * HALF
                v.scalar_tensor_tensor(W[:, bass.ds(o + HALF, HALF)], stage[:, k, :], WSCALE, W[:, bass.ds(o, HALF)],
                                       ALU.mult, ALU.subtract).then_inc(s_cvl, 1)

            l3 = logits[:, :].rearrange("p (t e) -> p t e", e=E)
            lanes = lambda z: z.rearrange("p (t e) -> p t e", e=E)
            by_expert = rev_e[:, :].unsqueeze(1).broadcast_to([P, NT, E])
            s4, d4 = (z.rearrange("p (k n) -> p k n", k=TOPK) for z in (selk, prodk))
            dke = prodk.rearrange("p (i e) -> p i e", e=E)

            def biased_logits():
                dve.wait_ge(s_lgf, B)
                dve.wait_ge(s_const, CONSTS)
                v.tensor_tensor(lanes(lrb), l3, rb_sb[:, :].unsqueeze(1).broadcast_to([P, NT, E]), ALU.add).then_inc(s_lrb, 1)

            def probabilities():
                dve.wait_ge(s_ex, 1)
                link(v.tensor_scalar(pr, pr, 1.0, None, ALU.add))
                link(v.reciprocal(pr, pr))

            def choose(k):
                left = (pr, pr2)[k]
                top, one = topv[:, k * NT:(k + 1) * NT], selk[:, k * TE:(k + 1) * TE]
                link(v.tensor_reduce(top, lanes(left), AX_X, ALU.max))
                link(v.tensor_tensor(lanes(eqv), lanes(left), top.unsqueeze(2).broadcast_to([P, NT, E]), ALU.is_equal))
                link(v.tensor_tensor(lanes(eqv), lanes(eqv), by_expert, ALU.mult))
                link(v.tensor_reduce(best, lanes(eqv), AX_X, ALU.max))
                link(v.tensor_tensor(lanes(one), by_expert, best.unsqueeze(2).broadcast_to([P, NT, E]), ALU.is_equal))
                if k == 0:
                    link(v.scalar_tensor_tensor(pr2, one, -2.0, pr, ALU.mult, ALU.add))
                else:
                    v.tensor_tensor(sel16, selk[:, 0:TE], one, ALU.add).then_inc(s_sel, 1)

            def gate_weights():
                link(v.tensor_tensor(vsum, topv[:, 0:NT], topv[:, NT:KT_N], ALU.add))
                link(v.reciprocal(vinv, vsum))
                wk3 = wk_f.rearrange("p (k t) -> p k t", k=TOPK)
                link(v.tensor_tensor(wk3, topv.rearrange("p (k t) -> p k t", k=TOPK), vinv.unsqueeze(1).broadcast_to([P, TOPK, NT]), ALU.mult))
                link(v.tensor_copy(whi, wk_f))
                link(v.tensor_tensor(wlo, wk_f, whi, ALU.subtract))

            def slots():
                dve.wait_ge(s_pos, 1)
                link(v.tensor_tensor(cgt.rearrange("p (e c) -> p e c", e=E), RB[:, TE:TE + E].unsqueeze(2).broadcast_to([P, E, NT]),
                                     cnt_iota[:, :].unsqueeze(1).broadcast_to([P, E, NT]), ALU.is_gt))
                link(v.tensor_reduce(nblk, cgt.rearrange("p (e c) -> p e c", e=E), AX_X, ALU.add))
                link(v.tensor_tensor(endm.rearrange("p (e f) -> p e f", e=E), tri_le[:, :, :], nblk.unsqueeze(1).broadcast_to([P, E, E]), ALU.mult))
                link(v.tensor_reduce(endb, endm.rearrange("p (e f) -> p e f", e=E), AX_X, ALU.add))
                link(v.tensor_tensor(startb, endb, nblk, ALU.subtract))
                link(v.scalar_tensor_tensor(lanes(slot_te), startb.unsqueeze(1).broadcast_to([P, NT, E]), float(P),
                                            lanes(RB[:, 0:TE]), ALU.mult, ALU.add))
                link(v.tensor_tensor(d4, s4, slot_te.unsqueeze(1).broadcast_to([P, TOPK, TE]), ALU.mult))
                link(v.tensor_reduce(slotk, dke, AX_X, ALU.add))
                link(v.tensor_copy(slot_i, slotk))
                link(v.tensor_scalar(lane_i, slot_i, P - 1, None, ALU.bitwise_and))
                link(v.tensor_scalar(blk_i, slot_i, P.bit_length() - 1, None, ALU.arith_shift_right))

            def lane_onehots(k):
                own = slice(k * NT, (k + 1) * NT)
                v.tensor_tensor(lane1h[:, own, :], lane_i[:, own].unsqueeze(2).broadcast_to([P, NT, P]),
                                lane_iota[:, :].unsqueeze(1).broadcast_to([P, NT, P]), ALU.is_equal).then_inc(s_1h, 1)

            def block_onehots():
                v.tensor_tensor(blk1h[:, :, 0, :], blk_i.unsqueeze(2).broadcast_to([P, KT_N, NR]),
                                lane_iota[:, 0:NR].unsqueeze(1).broadcast_to([P, KT_N, NR]), ALU.is_equal).then_inc(s_b1h, 1)

            def block_experts():
                link(v.tensor_tensor(lanes(eb_m[0:1, :]), endb[0:1, :].unsqueeze(1).broadcast_to([1, NR, E]),
                                     lane_iota[0:1, 0:NR].unsqueeze(2).broadcast_to([1, NR, E]), ALU.is_le))
                link(v.tensor_reduce(eb_f[0:1, :], lanes(eb_m[0:1, :]), AX_X, ALU.add))
                link(v.tensor_scalar(eoff[0:1, NT:NB], eb_f[0:1, :], float(E - 1), float(SLOT), ALU.min, ALU.mult))

            def tables():
                dve.wait_ge(s_tab, 1)
                occ, tid, th, tl = (RB[:, f * NR:(f + 1) * NR] for f in range(4))
                link(v.tensor_copy(tok[:, :], tid))
                link(v.tensor_scalar(tgt_f, occ, pad_neg[:, 0:1], pad_row[:, 0:1], ALU.mult, ALU.add))
                link(v.tensor_tensor(tgt[:, NT:NB], tgt_f, tid, ALU.add))
                link(v.tensor_scalar(w_f, th, gff[:, 0:1], None, ALU.mult))
                v.scalar_tensor_tensor(wcol[:, NT:NB], tl, gff[:, 0:1], w_f, ALU.mult, ALU.add).then_inc(s_route, 1)

            def routing_at(n):
                if n == 2:
                    probabilities()
                    choose(0)
                elif n == 3:
                    choose(1)
                    gate_weights()
                elif n == POS_BLOCK:
                    slots()
                elif n == 5:
                    block_onehots()
                    block_experts()
                elif n in (6, 7):
                    lane_onehots(n - 6)
                elif n == TAB_BLOCK:
                    tables()

            def xT_lo(n):
                dve.wait_ge(s_xth, n - NT + 1)
                v.tensor_tensor(xT[:, LO, :], PXT[:, :], xT[:, HI, :], ALU.subtract).then_inc(s_xtl, 1)

            def gated(n):
                dve.wait_ge(s_silu, n + 1)
                need(dve, s_ht, n)
                v.tensor_tensor(h[:, 0:H], PU[:, 0:H], silu_g[:, :], ALU.mult).then_inc(s_h, 1)

            def hT_lo(n):
                dve.wait_ge(s_hth, n + 1)
                v.tensor_tensor(hT[:, LO, :], PHT[:, 0:HC * P], hT[:, HI, :], ALU.subtract).then_inc(s_htl, 1)

            def blk(n, turn=False):
                gated(n)
                if turn:
                    xT_lo(n + 1)
                hT_lo(n)

            for q in range(NQ):
                x_stats(0, q)
            x_moments(0)
            parameters()
            step(None, 0, 1)
            for k in (1, 0):
                convert(SHARED_AT, k, s_shh[k], 0)
            with dve.Fori(0, B - 2) as b:
                step(b, b + 1, b + 2)
            step(B - 2, B - 1, None)
            step(B - 1, None, None)
            biased_logits()
            routed_half(2)
            hT_lo(1)
            for n in range(2, PEELED):
                gated(n)
                routing_at(n)
                hT_lo(n)
                routed_half(n + 1)
            with dve.Fori(PEELED // 2, NT // 2 - 1) as r:
                for k in range(2):
                    blk(2 * r + 1 + k)
                    convert((r + 1) * SLOT, k, s_cvh, 2 * r + 2 + k)
            blk(NT - 1, turn=True)
            with dve.Fori(NT // 2, (NB - 1) // 2) as r:
                for i in range(2):
                    blk(2 * r + i, turn=True)
            blk(NB - 1)

        @block.tensor
        def _(pe):
            t = nc.tensor

            def transposes(bank, src, count, s):
                for c in range(count):
                    last = t.transpose(bank[:, c * P:(c + 1) * P], src(c), ident[:, :])
                last.then_inc(s, 1)

            pe.wait_ge(s_const, CONSTS)

            def turn_context(b):
                pe.wait_ge(s_ctx, 16 * (b + 1))
                for c in range(CC):
                    need(pe, s_ef, 8 * b + c - 1)
                    transposes(EB[c], lambda n: ctx_sb[:, n, c * P:(c + 1) * P], NQ, s_eb)

            def project(b, m, between=None):
                pe.wait_ge(s_ef, 8 * b + CC)
                for c in range(CC):
                    if c == CC - 1 and between is not None:
                        between()
                    last = t.matmul(EB[m][:, :], wqkT[:, m, c, :], ctxT[:, c, :], start=(c == 0), stop=(c == CC - 1))
                last.then_inc(s_eb, 1)

            def energy(b, q):
                pe.wait_ge(s_ef, 8 * b + max(4, 3 + q))
                t.matmul(EB[q % 2][:, :], qT[:, q * P:(q + 1) * P], kT, start=True, stop=True).then_inc(s_eb, 1)

            def turn_xn(b, q):
                pe.wait_ge(s_xn, NQ * b + q + 1)
                need(pe, s_xnl, NQ * b + q)
                transposes(TPX, lambda c: xn[:, q % 2, c * P:(c + 1) * P], DC, s_xnt)

            def turn_probs(b, q):
                pe.wait_ge(s_pn, NQ * b + q + 1)
                need(pe, s_pl, NQ * b + q)
                transposes(TPP, lambda c: prob[:, q % 2, c * P:(c + 1) * P], DC, s_pt)

            def turn_x2(b, q):
                pe.wait_ge(s_x2n, NQ * b + q + 1)
                if q in (1, NQ - 1):
                    pe.wait_ge(s_x2l, NQ * b + min(q, NQ - 2))
                transposes(x2_bank(q), lambda c: x2n[:, q % 2, c * P:(c + 1) * P], DC, s_xt2)

            def attend(b, q):
                if q == 0:
                    pe.wait_ge(s_xnl, NQ * (b + 1))
                    pe.wait_ge(s_pl, NQ * (b + 1))
                two_before(pe, s_x2, b, q)
                bank = XM[q % 2]
                for c in range(DC):
                    chunk = xnt(b, HI, q, c)
                    t.matmul(bank[:, :], chunk, att(b, HI, c), start=(c == 0), stop=False)
                    t.matmul(bank[:, :], chunk, att(b, LO, c), start=False, stop=False)
                    last = t.matmul(bank[:, :], xnt(b, LO, q, c), att(b, HI, c), start=False, stop=(c == DC - 1))
                last.then_inc(s_xm, 1)

            def route_logits(b, q):
                pe.wait_ge(s_x2l, NQ * b + q + 1)
                dst = LG[:, q * E:(q + 1) * E]
                for c in range(DC):
                    hi, lo = (xT2_chunk(NQ * b + q, l, c) for l in (HI, LO))
                    t.matmul(dst, hi, wr16[:, HI, c, :], start=(c == 0), stop=False)
                    t.matmul(dst, hi, wr16[:, LO, c, :], start=False, stop=False)
                    last = t.matmul(dst, lo, wr16[:, HI, c, :], start=False, stop=(c == DC - 1))
                last.then_inc(s_lg, 1)

            def step(s2, s1, nx):
                for q in range(NQ):
                    if s1 is not None:
                        energy(s1, q)
                        turn_xn(s1, q)
                        if q > 0:
                            turn_probs(s1, q - 1)
                    elif q == 1:
                        turn_h(0)
                    if s2 is not None:
                        attend(s2, q)
                        if q > 1:
                            turn_x2(s2, q - 2)
                        if q > 2 and nx is None:
                            route_logits(s2, q - 3)
                n = 0 if s1 is not None else 1
                if nx is not None:
                    turn_context(nx)
                    if s2 is not None:
                        route_logits(s2, NQ - 4)
                    turn_probs(s1, NQ - 1)
                    project(nx, 0, (lambda: turn_x2(s2, NQ - 2)) if s2 is not None else None)
                    if s2 is not None:
                        route_logits(s2, NQ - 3)
                        turn_x2(s2, NQ - 1)
                    project(nx, 1, (lambda: route_logits(s2, NQ - 2)) if s2 is not None else None)
                else:
                    if s1 is not None:
                        turn_probs(s1, NQ - 1)

                    def last_turn():
                        if s1 is None:
                            pe.wait_ge(s_x2, NT)
                            down(0, SHARED_AT)
                        turn_x2(s2, NQ - 1)

                    gate_up(n, SHARED_AT, own=n, before={1 + n: lambda: turn_x2(s2, NQ - 2), DC - 1: last_turn})
                    route_logits(s2, NQ - 3)
                    route_logits(s2, NQ - 2)
                if s2 is not None:
                    route_logits(s2, NQ - 1)

            def positions():
                pe.wait_ge(s_sel, 1)
                t.matmul(RB[:, 0:TE], tri16[:, :], sel16, start=True, stop=False, skip_group_check=True)
                for j in range(NT):
                    rest = NT - j
                    last = t.matmul(RB[:, (j + 1) * E:(NT + 1) * E].rearrange("p (r e) -> p r e", e=E), ones16[:, :],
                                    sel16[:, j * E:(j + 1) * E].unsqueeze(1).broadcast_to([P, rest, E]),
                                    start=False, stop=(j == NT - 1), skip_group_check=True)
                last.then_inc(s_pos, 1)

            def table_rows():
                pe.wait_ge(s_1h, TOPK)
                pe.wait_ge(s_bf, 3)
                table = RB[:, 0:4 * NR]
                for i in range(KT_N):
                    last = t.matmul(table, lane1h[:, i, :], blk1h[:, i, :, :].rearrange("p f n -> p (f n)"),
                                    start=(i == 0), stop=(i == KT_N - 1))
                last.then_inc(s_tab, 1)

            def gate_up(n, off, own=None, before={}):
                if own is None:
                    pe.wait_ge(s_xtl, n - NT + 1)
                for c in range(DC):
                    if c in before:
                        before[c]()
                    if own is None:
                        hi, lo = (xT[:, l, c * P:(c + 1) * P] for l in (HI, LO))
                    else:
                        hi, lo = (xT2_chunk(own, l, c) for l in (HI, LO))
                    for m, bank in enumerate((PG, PU)):
                        t.matmul(bank[:, 0:H], hi, gu_w(off, HI, m, c), start=(c == 0), stop=False)
                        t.matmul(bank[:, 0:H], hi, gu_w(off, LO, m, c), start=False, stop=False)
                    for m, bank in enumerate((PG, PU)):
                        last = t.matmul(bank[:, 0:H], lo, gu_w(off, HI, m, c), start=False, stop=(c == DC - 1))
                last.then_inc(s_gu, 1)

            def down(n, off):
                pe.wait_ge(s_htl, n + 1)
                need(pe, s_y, n)
                for j in range(HC):
                    hi, lo = (hT[0:HK[j], l, j * P:(j + 1) * P] for l in (HI, LO))
                    t.matmul(PY[:, :], hi, dn_w(off, HI, j), start=(j == 0), stop=False)
                    t.matmul(PY[:, :], hi, dn_w(off, LO, j), start=False, stop=False)
                    last = t.matmul(PY[:, :], lo, dn_w(off, HI, j), start=False, stop=(j == HC - 1))
                last.then_inc(s_dn, 1)

            def turn_x(n, i, gathered):
                pe.wait_ge(s_xg[i], 16 * gathered)
                transposes(PXT, lambda c: xg[:, i, c * P:(c + 1) * P], DC, s_xt)

            def blk(n, i, gathered, off, before):
                gate_up(n, off)
                if gathered is not None:
                    turn_x(n + 1, 1 - i, gathered)
                down(n - 1, before)
                turn_h(n)

            def shared_blk(n, beside=None):
                gate_up(n, SHARED_AT, own=n)
                if beside is not None:
                    beside()
                down(n - 1, SHARED_AT)
                turn_h(n)

            def turn_h(n):
                pe.wait_ge(s_h, n + 1)
                transposes(PHT, lambda c: h[:, c * P:(c + 1) * P], HC, s_ht)

            def expert(n):
                return pe.value_load(eoff[0:1, bass.ds(n, 1)], min_val=0, max_val=SHARED_AT)

            turn_context(0)
            pe.wait_ge(s_wqk, 16 * 2)
            transposes(RB, lambda c: wqk[:, c // CC, c % CC * P:(c % CC + 1) * P], 2 * CC, s_wT)
            pe.wait_ge(s_wTc, 1)
            project(0, 0)
            project(0, 1)
            step(None, 0, 1)
            pe.wait_ge(s_wrl, 1)
            with pe.Fori(0, B - 2) as b:
                step(b, b + 1, b + 2)
            pe.wait_ge(s_cvl, 2)
            step(B - 2, B - 1, None)
            step(B - 1, None, None)
            turn_h(1)
            for n in range(2, PEELED):
                shared_blk(n, positions if n == POS_BLOCK else table_rows if n == TAB_BLOCK else None)
            with pe.Fori(PEELED // 2, NT // 2 - 1) as r:
                for k in range(2):
                    shared_blk(2 * r + 1 + k)
            shared_blk(NT - 1, lambda: turn_x(NT, 0, 1))
            pe.wait_ge(s_route, 1)
            pe.wait_ge(s_cvl, 2 + 2 * E)
            PER_TURN = 12
            turns = (NB - NT) // PER_TURN
            with pe.Fori(0, turns) as r:
                before = expert(PER_TURN * r + (NT - 1))
                for k in range(PER_TURN):
                    off = expert(PER_TURN * r + (NT + k))
                    blk(PER_TURN * r + (NT + k), k % 2, PER_TURN // 2 * r + ((k + 1) // 2 + 1), off, before)
                    before = off
            before = expert(NT + PER_TURN * turns - 1)
            for n in range(NT + PER_TURN * turns, NB):
                off = expert(n)
                blk(n, n % 2, (n + 1 - NT) // 2 + 1 if n < NB - 1 else None, off, before)
                before = off
            down(NB - 1, before)


_INS = ["x", "ctx_1024", "g_xattn", "g_ffn", "L0_xattn_Wq", "L0_xattn_bq", "L0_xattn_Wk", "L0_xattn_bk",
        "L0_ffn_Wg_s", "L0_ffn_Wu_s", "L0_ffn_Wd_s", "L0_ffn_Wg", "L0_ffn_Wu", "L0_ffn_Wd",
        "L0_ffn_Wr", "L0_ffn_br", "L0_ffn_rb"]


def kernel(**inputs):
    import numpy as np
    import concourse.bacc as bacc
    from concourse.bass_utils import run_bass_kernel_spmd

    nc = bacc.Bacc("TRN2", target_bir_lowering=False, num_devices=1)
    arrays, args = {}, []
    for name in _INS:
        a = np.ascontiguousarray(inputs[name])
        arrays[f"in_{name}"] = a
        args.append(nc.dram_tensor(f"in_{name}", a.shape, mybir.dt.from_np(a.dtype), kind="ExternalInput").ap())
    b, s, d = inputs["x"].shape
    out = nc.dram_tensor("out_rows", (b * s + P, d), F32, kind="ExternalOutput").ap()
    flamingo_block(nc, *args, out)
    got = run_bass_kernel_spmd(nc, [arrays], core_ids=[0]).results[0]["out_rows"]
    return got[:b * s].reshape(b, s, d)
```
